# Optimizing a Trainium2 kernel written in Bass

```python
import numpy as np
import jax
import jax.numpy as jnp

def _softmax(x, axis=-1):
    return jax.nn.softmax(x, axis=axis)

def _gelu(x):
    return jax.nn.gelu(x, approximate=True)

def _silu(x):
    return jax.nn.silu(x)

def _sigmoid(x):
    return jax.nn.sigmoid(x)

def _layernorm(x, axis=-1, eps=1e-05):
    m = jnp.mean(x, axis=axis, keepdims=True)
    v = jnp.var(x, axis=axis, keepdims=True)
    return (x - m) / jnp.sqrt(v + eps)

def _scatter_add(tgt, idx, src, axis=0):
    return tgt.at[idx].add(src)

def _segment_sum(src, seg, n):
    return jax.ops.segment_sum(src, seg, n)
kernel_name = 'mk_cond_resid_d4_seqx_r4_f276be'

def setup_inputs(seed: int=0):
    np.random.seed(seed)
    _w = jnp.asarray

    def _rec_inputs():
        import jax
        import jax.numpy as jnp
        _rk = jax.random.key(seed)
        x = -7.109e-05 + 0.9999 * jax.random.normal(jax.random.fold_in(_rk, 1), (32, 64, 1024), jnp.float32)
        _lenS = 64 - jax.random.randint(jax.random.fold_in(_rk, 7), (32,), 0, max(1, 64 // 4) + 1, jnp.int32)
        _lenS2 = 64 - jax.random.randint(jax.random.fold_in(_rk, 8), (32,), 0, max(1, 64 // 4) + 1, jnp.int32)
        itok_B_0_15 = jax.random.randint(jax.random.fold_in(_rk, 11), (32,), 0, 16, jnp.int32)
        itok_B_0_2 = jax.random.randint(jax.random.fold_in(_rk, 12), (32,), 0, 3, jnp.int32)
        itok_B_3_7 = jax.random.randint(jax.random.fold_in(_rk, 13), (32,), 3, 8, jnp.int32)
        return (x, itok_B_0_15, itok_B_0_2, itok_B_3_7)
    x, itok_B_0_15, itok_B_0_2, itok_B_3_7 = _rec_inputs()

    def _L0_cond_setup():
        import jax, jax.numpy as jnp
        import numpy as np
        NUM_CONDITIONS = 16
        IN_CH = 64
        OUT_CH = 64
        B = 64
        T = 1024
        key = jax.random.key(seed)
        k_x, k_w, k_c = jax.random.split(key, 3)
        x = jax.random.normal(k_x, (B, IN_CH, T), dtype=jnp.float32)
        bound = float(np.sqrt(6.0 / IN_CH))
        weights = jax.random.uniform(k_w, (NUM_CONDITIONS, IN_CH, OUT_CH), dtype=jnp.float32, minval=-bound, maxval=bound)
        condition = jax.random.randint(k_c, (B,), 0, NUM_CONDITIONS, dtype=jnp.int64)
        return {'x': x, 'weights': weights, 'condition': condition}
    _L0_cond_all = _L0_cond_setup()
    _L0_cond_in = {k: v for k, v in _L0_cond_all.items() if k in ('weights',)}
    del _L0_cond_all

    def _L1_cond_setup():
        import jax, jax.numpy as jnp
        import numpy as np
        B, C, T = (64, 64, 1024)
        S, D = (16, 64)
        key = jax.random.key(seed)
        k1, k2, k3 = jax.random.split(key, 3)
        x = jax.random.normal(k1, (B, C, T), dtype=jnp.float32)
        condition = jax.random.randint(k2, (B,), 0, S, dtype=jnp.int64)
        bound = float(np.sqrt(6.0 / C))
        weights = jax.random.uniform(k3, (S, C, D), dtype=jnp.float32, minval=-bound, maxval=bound)
        return {'x': x, 'condition': condition, 'weights': weights}
    _L1_cond_all = _L1_cond_setup()
    _L1_cond_in = {k: v for k, v in _L1_cond_all.items() if k in ('weights',)}
    del _L1_cond_all

    def _L2_cond_setup():
        import jax, jax.numpy as jnp
        import numpy as np
        B, S, D_IN, D_OUT = (4, 512, 1024, 1024)
        R, NUM_LABELERS = (32, 5)
        LORA_SCALING = 16 / 32
        key = jax.random.key(seed)
        k1, k2, k3, k4, k5 = jax.random.split(key, 5)
        x = jax.random.normal(k1, (B, S, D_IN), dtype=jnp.float32)
        labeler_index = jax.random.randint(k2, (B,), 0, NUM_LABELERS, dtype=jnp.int64)
        W = jax.random.normal(k3, (D_OUT, D_IN), dtype=jnp.float32) * 0.02
        lora_A = jax.random.normal(k4, (NUM_LABELERS, D_IN, R), dtype=jnp.float32) * 0.02
        lora_B_w = jax.random.normal(k5, (D_OUT, R), dtype=jnp.float32) * 0.02
        return {'x': x, 'labeler_index': labeler_index, 'W': W, 'lora_A': lora_A, 'lora_B_w': lora_B_w}
    _L2_cond_all = _L2_cond_setup()
    _L2_cond_in = {k: v for k, v in _L2_cond_all.items() if k in ('W', 'lora_A', 'lora_B_w')}
    del _L2_cond_all

    def _L3_cond_setup():
        import jax, jax.numpy as jnp
        import numpy as np
        MAX_LORAS, OUT, IN = (8, 1024, 1024)
        B, S = (4, 512)
        key = jax.random.key(seed)
        k1, k2, k3 = jax.random.split(key, 3)
        x = jax.random.normal(k1, (B, S, IN), dtype=jnp.float32)
        weight = jax.random.normal(k2, (MAX_LORAS, OUT, IN), dtype=jnp.float32) * 0.02
        adapter_ids = jax.random.randint(k3, (B,), 0, MAX_LORAS, dtype=jnp.int32)
        return {'x': x, 'weight': weight, 'adapter_ids': adapter_ids}
    _L3_cond_all = _L3_cond_setup()
    _L3_cond_in = {k: v for k, v in _L3_cond_all.items() if k in ('weight',)}
    del _L3_cond_all
    return {'x': x, 'itok_B_0_15': itok_B_0_15, 'itok_B_0_2': itok_B_0_2, 'itok_B_3_7': itok_B_3_7, 'L0_cond_weights': _L0_cond_in['weights'], 'L1_cond_weights': _L1_cond_in['weights'], 'L2_cond_W': _L2_cond_in['W'], 'L2_cond_lora_A': _L2_cond_in['lora_A'], 'L2_cond_lora_B_w': _L2_cond_in['lora_B_w'], 'L3_cond_weight': _L3_cond_in['weight']}

def reference(x, itok_B_0_15, itok_B_0_2, itok_B_3_7, L0_cond_weights, L1_cond_weights, L2_cond_W, L2_cond_lora_A, L2_cond_lora_B_w, L3_cond_weight):
    import jax
    import jax.numpy as jnp

    def _L0_cond_ref(x, weights, condition):
        import jax, jax.numpy as jnp
        import numpy as np
        NUM_CONDITIONS = 16
        IN_CH = 64
        OUT_CH = 64
        B = 64
        T = 1024
        W = weights[condition]
        return jnp.einsum('bct,bcd->bdt', x, W)

    def _L1_cond_ref(x, condition, weights):
        import jax, jax.numpy as jnp
        import numpy as np
        B, C, T = (64, 64, 1024)
        S, D = (16, 64)
        W = weights[condition]
        return jnp.einsum('bct,bcd->bdt', x, W)

    def _L2_cond_ref(x, labeler_index, W, lora_A, lora_B_w):
        import jax, jax.numpy as jnp
        import numpy as np
        B, S, D_IN, D_OUT = (4, 512, 1024, 1024)
        R, NUM_LABELERS = (32, 5)
        LORA_SCALING = 16 / 32
        base = jnp.einsum('bsi,oi->bso', x, W)
        labelers_A = lora_A[labeler_index]
        low = jnp.einsum('bsi,bir->bsr', x, labelers_A)
        delta = jnp.einsum('bsr,or->bso', low, lora_B_w) * LORA_SCALING
        return base + delta

    def _L3_cond_ref(x, weight, adapter_ids):
        import jax, jax.numpy as jnp
        import numpy as np
        MAX_LORAS, OUT, IN = (8, 1024, 1024)
        B, S = (4, 512)
        w = weight[adapter_ids]
        return jnp.einsum('bsi,boi->bso', x, w)
    x = x + _L0_cond_ref(x, L0_cond_weights, itok_B_0_15)
    x = x + _L1_cond_ref(x, itok_B_0_15, L1_cond_weights)
    x = x + _L2_cond_ref(x, itok_B_0_2, L2_cond_W, L2_cond_lora_A, L2_cond_lora_B_w)
    x = x + _L3_cond_ref(x, L3_cond_weight, itok_B_3_7)
    return x

_drawn_inputs = setup_inputs


def setup_inputs(seed=0):
    import zlib

    import numpy as np

    out = dict(_drawn_inputs(seed))
    spreads = {}
    factors = {}
    for name, (base, spread) in spreads.items():
        noise = np.random.default_rng([zlib.crc32(name.encode()), seed]).standard_normal(out[name].shape)
        drawn = base * np.exp(spread * noise) if base else spread * noise
        out[name] = jnp.asarray(drawn.astype(out[name].dtype))
    for name, factor in factors.items():
        out[name] = (out[name] * factor).astype(out[name].dtype)
    return out
```

```python
import numpy as np
import concourse.bass as bass
from concourse import mybir

F32 = mybir.dt.float32
F32R = mybir.dt.float32r
I32 = mybir.dt.int32
ALU = mybir.AluOpType
ACT = mybir.ActivationFunctionType
AX = mybir.AxisListType

P = 128
B, T, D = 32, 64, 1024
NC_, NL, R, NA = 16, 5, 32, 8
KT = D // P
PAIRS = B // 2
CH = 4
CT = B * T // CH
CB = B // CH
CP = PAIRS // CH
SLOTS = B // 2 + NA // 2
SURE = B // 2
RAW = 4
RING = 12
UNIT = 2 * D
HALF = KT // 2
LW = KT * 2 * R + 2 * R

(TOK0, TOK1, ROW0, ROW1, LOAD_A, LOAD_B, NEXT8, NEXT_OFF_A, NEXT_OFF_B, THIS8, OFF_A, OFF_B) = range(12)
FIELDS = 12
N_SLOTS, N_ACTIVE, ADAPTER = 0, 1, 2
HEAD = 16
C_E, C_S, C_B, C_LT8 = 0, NA, NA + SLOTS, NA + SLOTS + B
C_SIZE = C_LT8 + NA * NA


def constants():
    small = np.zeros((1, C_SIZE), np.float32)
    small[0, C_E:C_E + NA] = np.arange(NA)
    small[0, C_S:C_S + SLOTS] = np.arange(SLOTS)
    small[0, C_B:C_B + B] = np.arange(B)
    small[0, C_LT8:] = np.tril(np.ones((NA, NA), np.float32), -1).ravel()
    before = np.tril(np.ones((B, B), np.float32), -1).reshape(1, B * B)
    eye = np.eye(P, dtype=np.float32)
    eye2 = np.concatenate([np.eye(T, dtype=np.float32)] * 2, axis=1)
    return small, before, eye, eye2


def build(nc, x, cond, labeler, adapter, w0t, w1, wt, lora_a, lora_b, w3t, small_c, before_c, eye_c, eye2_c, out):
    at = [1152]

    def sb(name, shape, dtype, offset=None):
        size = 4 * int(np.prod(shape[1:]))
        if offset is None:
            offset = at[0]
            at[0] += (size + 31) // 32 * 32
        return nc.alloc_sbuf_tensor_at(name, shape, dtype, offset=offset)

    xT_at = at[0]
    xT = sb("xT", [P, KT, B * T], F32)
    aT = sb("aT", [P, KT, 2, CT], F32R)
    ring_at = at[0]
    ring = sb("ring", [P, RING * UNIT], F32R)
    raw = sb("raw", [P, RAW, D], F32)
    eye = sb("eye", [P, P], F32)
    eye2 = sb("eye2", [T, 2 * T], F32)
    plan = sb("plan", [1, HEAD + SLOTS * FIELDS], I32)
    toks = sb("toks", [1, 3, B], I32)
    stage_at = at[0]
    stage = sb("stage", [P, 2, D], F32)
    mix_tab = sb("mix_tab", [P, NC_ * T], F32, offset=stage_at)
    mix_bd = sb("mix_bd", [P, 2 * CP, P], F32, offset=stage_at + 4 * NC_ * T)
    s_at = ring_at + 4 * UNIT * KT
    a_sel = sb("a_sel", [P, CB, LW], F32R, offset=s_at)
    s_at += 4 * CB * LW
    b_hi = sb("b_hi", [P, D], F32R, offset=s_at)
    b_lo = sb("b_lo", [P, D], F32R, offset=s_at + 4 * D)
    low_s = sb("low_s", [P, CT], F32R, offset=s_at + 8 * D)
    low_f = sb("low_f", [P, CT], F32, offset=s_at + 8 * D + 4 * CT)
    a_raw = sb("a_raw", [P, 2, KT * R], F32, offset=s_at + 8 * D + 8 * CT)
    assert s_at + 8 * D + 8 * CT + 8 * KT * R <= ring_at + 4 * UNIT * RING
    late = lambda k: xT[:, k, 2 * CT:4 * CT]
    small = xT[0:1, 0, 2 * CT:4 * CT]
    before = xT[0:1, 1, 2 * CT:4 * CT]
    w1_s = xT[0:T, 2, 2 * CT:4 * CT]
    w0_s = [xT[0:T, 3 + h, 2 * CT:4 * CT] for h in range(2)]
    b_raw = late(5)
    tmp = [xT[0:1, 6 + i, 2 * CT:4 * CT] for i in range(2)]

    def unit(g, part):
        return ring[:, g * UNIT + part * D:g * UNIT + (part + 1) * D]

    ps = [nc.alloc_psum_tensor(f"ps{i}", [P, 2, 512], F32) for i in range(4)]
    ps_mix, ps_low, ps_l2 = ps[0:2], ps[2], ps[3]

    sem = {}

    def s(name):
        if name not in sem:
            sem[name] = nc.alloc_semaphore(name)
        return sem[name]

    raw_seq = [("x", p) for p in range(CP)] + [("w", u) for u in range(KT)] + [("x", p) for p in range(CP, PAIRS)]
    raw_of = {e: n for n, e in enumerate(raw_seq)}
    assert len(raw_seq) % RAW == 0

    def wait_raw(eng, entry):
        n = raw_of[entry]
        eng.wait_ge(s(f"raw{n % RAW}"), 16 * (n // RAW + 1))

    def raw_tile(entry):
        return raw[:, raw_of[entry] % RAW, :]

    def w_unit(u):
        return u // 2, u % 2

    def w_diagonals(u):
        q, h = w_unit(u)
        return [k for k in (2 * q, 2 * q + 1) if k // HALF == h]

    def w_dst(u, part):
        q, h = w_unit(u)
        v = ring[:, :].rearrange("p (g t n) -> p g t n", t=2, n=D)
        return v[:, HALF * h:HALF * (h + 1), part, 256 * q:256 * (q + 1)]

    def record(eng, slot, field, lo, hi):
        i = HEAD + slot * FIELDS + field
        return eng.value_load(plan[0:1, i:i + 1], min_val=lo, max_val=hi)

    def head(eng, i, lo, hi):
        return eng.value_load(plan[0:1, i:i + 1], min_val=lo, max_val=hi)

    def slot_steps(eng, body, last=SLOTS):
        n = head(eng, N_SLOTS, SURE, SLOTS)
        for i in range(last):
            if i < SURE:
                body(i)
            else:
                with eng.If(n > i):
                    body(i)

    BEFORE3 = 8 * CH

    with nc.Block() as block:

        @block.sync
        def _(sp):
            xp = x.rearrange("(q two) t d -> q (two t) d", two=2)
            wv = wt.rearrange("(k p) o -> p k o", p=P)

            def raw_free(n):
                if n >= RAW:
                    kind, i = raw_seq[n - RAW] if n - RAW < len(raw_seq) else ("a", n - RAW - len(raw_seq))
                    if kind == "x":
                        sp.wait_ge(s("mixed"), i + 1)
                    else:
                        sp.wait_ge(s("w_lo"), i + 1 if kind == "w" else KT + i + 1)

            def load_raw(entry):
                n = raw_of[entry]
                raw_free(n)
                kind, i = entry
                if kind == "x":
                    dst, src = raw[:, n % RAW, :], xp[i, :, :]
                else:
                    q, h = w_unit(i)
                    dst = raw[:, n % RAW, :].rearrange("p (k o) -> p k o", k=HALF)
                    src = wv[:, HALF * h:HALF * (h + 1), 256 * q:256 * (q + 1)]
                sp.dma_start(dst, src).then_inc(s(f"raw{n % RAW}"), 16)

            def load_a(b):
                if b >= 2:
                    sp.wait_ge(s("a_lo"), b - 1)
                l = sp.value_load(toks[0:1, 1, b:b + 1], min_val=0, max_val=NL - 1)
                sp.dma_start(a_raw[:, b % 2, :], lora_a[bass.ds(l, 1), :, :].rearrange("a p n -> p (a n)"))\
                  .then_inc(s(f"a_raw{b % 2}"), 16)

            for e in raw_seq[0:2]:
                load_raw(e)
            for i, t in enumerate((cond, labeler, adapter)):
                sp.dma_start(toks[0:1, i, :], t).then_inc(s("toks"), 16)
            for e in raw_seq[2:6]:
                load_raw(e)
            sp.wait_ge(s("toks"), 48)
            for b in range(2):
                load_a(b)
            sp.dma_start(b_raw, lora_b).then_inc(s("b_raw"), 16)
            for e in raw_seq[6:8]:
                load_raw(e)
            for b in range(2, CB):
                load_a(b)
            for e in raw_seq[8:12]:
                load_raw(e)
            sp.dma_start(small[:, 0:C_SIZE], small_c).then_inc(s("consts"), 16)
            sp.dma_start(before, before_c).then_inc(s("consts"), 16)
            for c in range(1, CH):
                for j in range(CP):
                    load_raw(("x", c * CP + j))
                    load_a(c * CB + 2 * j)
                    load_a(c * CB + 2 * j + 1)
            sp.wait_ge(s("plan"), 1)
            n_active = head(sp, N_ACTIVE, 1, NA)
            for k in range(NA):
                def load_adapter():
                    e = head(sp, ADAPTER + k, 0, NA - 1)
                    for t in range(KT):
                        n = len(raw_seq) + KT * k + t
                        raw_free(n)
                        src = w3t[bass.ds(e, 1), t * P:(t + 1) * P, :].rearrange("a p n -> p (a n)")
                        sp.dma_start(raw[:, n % RAW, :], src).then_inc(s(f"raw{n % RAW}"), 16)
                if k == 0:
                    load_adapter()
                else:
                    with sp.If(n_active > k):
                        load_adapter()

        @block.gpsimd
        def _(pool):
            pool.memset(mix_bd[:, :, :], 0.0).then_inc(s("zeroed"), 1)
            pool.memset(a_sel[:, :, KT * 2 * R:LW].bitcast(F32), 0.0).then_inc(s("zeroed"), 1)
            pool.wait_ge(s("zeroed"), 2)
            pool.wait_ge(s("toks"), 48)
            pool.wait_ge(s("mix_tab"), 2)
            for p in range(PAIRS):
                if p >= 2 * CP:
                    pool.wait_ge(s("mixed"), p - 2 * CP + 1)
                for h in range(2):
                    c = pool.value_load(toks[0:1, 0, 2 * p + h:2 * p + h + 1], min_val=0, max_val=NC_ - 1)
                    rows = slice(h * T, (h + 1) * T)
                    pool.tensor_copy(mix_bd[rows, p % (2 * CP), h * T:(h + 1) * T],
                                     mix_tab[rows, bass.ds(c * T, T)]).then_inc(s("bd"), 1)

        @block.scalar
        def _(act):
            act.dma_start(eye[:, :], eye_c).then_inc(s("eye"), 16)
            act.dma_start(w1_s, w1).then_inc(s("w1"), 16)
            for h in range(2):
                act.dma_start(w0_s[h], w0t[:, h, :]).then_inc(s("w0"), 16)
            act.dma_start(eye2[:, :], eye2_c).then_inc(s("w0"), 16)

            act.wait_ge(s("mm"), 1)
            for h in range(2):
                act.activation(mix_tab[:, 512 * h:512 * (h + 1)], ps_mix[0][:, h, :], ACT.Copy).then_inc(s("mix_tab"), 1)

            def mix_out(p):
                act.wait_ge(s("mixed"), p + 1)
                if p == 2 * CP:
                    act.wait_ge(s("plan"), 1)
                    act.wait_ge(s("b_lo"), 1)
                act.activation(xT[:, :, P * p:P * (p + 1)],
                               ps_mix[p % 2][:, :, :].rearrange("p a (k n) -> p (a k) n", n=P), ACT.Copy)\
                   .then_inc(s("x2"), 1)

            def w_hi(u):
                if w_diagonals(u):
                    act.wait_ge(s("w_eye"), sum(len(w_diagonals(v)) for v in range(u + 1)))
                else:
                    wait_raw(act, ("w", u))
                act.activation(w_dst(u, 0), raw_tile(("w", u)).rearrange("p (k o) -> p k o", k=HALF), ACT.Copy)\
                   .then_inc(s("w_hi"), 1)

            def a_hi(c, k):
                act.wait_ge(s("x2"), CP * (c + 1))
                if c:
                    act.wait_ge(s("steps"), KT * (c - 1) + k + 1)
                act.activation(aT[:, k, 0, :], xT[:, k, CT * c:CT * (c + 1)], ACT.Copy).then_inc(s("x_hi"), 1)

            def lora_hi(b):
                act.wait_ge(s(f"a_raw{b % 2}"), 16 * (b // 2 + 1))
                act.wait_ge(s("low"), b // CB)
                act.activation(a_sel[:, b % CB, 0:KT * 2 * R].rearrange("p (k t r) -> p k t r", t=2, r=R)[:, :, 0, :],
                               a_raw[:, b % 2, :].rearrange("p (k r) -> p k r", r=R), ACT.Copy).then_inc(s("a_hi"), 1)

            def low_out(c):
                v = ps_low[:, :, :].rearrange("p a (b t n) -> p (a b) t n", t=2, n=T)
                act.wait_ge(s("low"), c + 1)
                act.activation(low_f[:, :].rearrange("p (b n) -> p b n", n=T), v[:, :, 1, :], ACT.Copy).then_inc(s("low_t"), 1)
                act.wait_ge(s("low_f"), c + 1)
                act.wait_ge(s("steps"), KT * c)
                act.activation(low_s[:, :], low_f[:, :], ACT.Copy).then_inc(s("low_hi"), 1)

            def l2_out(c, o):
                if o < KT - 1:
                    act.wait_ge(s("l2"), (KT - 1) * c + o + 1)
                else:
                    act.wait_ge(s("steps"), KT * (c + 1))
                act.activation(xT[:, o, CT * c:CT * (c + 1)], ps_l2[:, o % 2, :], ACT.Copy).then_inc(s("x3"), 1)

            for p in range(CP):
                mix_out(p)
                if p < 2:
                    w_hi(p)
            for k in range(KT):
                a_hi(0, k)
            for b in range(CB):
                lora_hi(b)
            w_hi(2)
            w_hi(3)
            act.wait_ge(s("b_raw"), 16)
            act.activation(b_hi[:, :], b_raw, ACT.Copy, scale=0.5).then_inc(s("b_hi"), 1)

            def adapter_hi(k, t, dst, count8):
                act.wait_ge(s("w_eye"), count8 + (t + 1))
                act.activation(dst, raw[:, t % RAW, :], ACT.Copy).then_inc(s("w_hi"), 1)

            for c in range(CH):
                low_out(c)
                if c == 0:
                    w_hi(4)
                    w_hi(5)
                l2_out(c, 0)
                l2_out(c, 1)
                if c == 0:
                    w_hi(6)
                    w_hi(7)
                for o in range(2, KT - 1):
                    l2_out(c, o)
                    if c + 1 < CH:
                        if o - 2 < CP:
                            mix_out(CP * (c + 1) + o - 2)
                        for b in range(2 * (o - 2), min(2 * (o - 1), CB)):
                            lora_hi(CB * (c + 1) + b)
                    elif o < 4:
                        act.wait_ge(s("low"), CH)
                        adapter_hi(0, o - 2, unit(KT + o - 2, 0), KT)
                if c + 1 < CH:
                    for k in range(KT):
                        a_hi(c + 1, k)
                else:
                    act.wait_ge(s("delta"), 1)
                    for t in range(2, HALF):
                        adapter_hi(0, t, unit(KT + t, 0), KT)
                    for t in range(HALF, KT):
                        act.wait_ge(s("steps"), KT * (CH - 1) + t - HALF + 1)
                        if t == KT - 1:
                            l2_out(c, KT - 1)
                        adapter_hi(0, t, unit(t - HALF, 0), KT)
                if c + 1 < CH:
                    l2_out(c, KT - 1)

            def slot_hi(i):
                act.wait_ge(s("steps"), BEFORE3 + KT * max(0, i - 3))
                for h in range(2):
                    tok = record(act, i, TOK0 + h, 0, (B - 1) * T)
                    col = (i % 4) * P + h * T
                    act.activation(aT[:, :, 0, col:col + T], xT[:, :, bass.ds(tok, T)], ACT.Copy).then_inc(s("s_hi"), 1)

            def slot_out(i):
                act.wait_ge(s("steps"), BEFORE3 + KT * (i + 1))
                if i >= 2:
                    act.wait_ge(s(f"stored{i - 2}"), 32)
                act.activation(stage[:, i % 2, :], ps[i % 4][:, :, :].rearrange("p a n -> p (a n)"), ACT.Copy)\
                   .then_inc(s("staged"), 1)
                act.wait_ge(s("staged"), i + 1)
                for h in range(2):
                    row = record(act, i, ROW0 + h, 0, B + SLOTS - 1)
                    act.dma_start(out[bass.ds(row, 1), :, :].rearrange("a t d -> (a t) d"),
                                  stage[h * T:(h + 1) * T, i % 2, :]).then_inc(s(f"stored{i}"), 16)

            act.wait_ge(s("plan"), 1)
            act.wait_ge(s("x3"), KT * CH)
            slot_hi(0)
            n_slots = head(act, N_SLOTS, SURE, SLOTS)

            def prefetch(i):
                load_a = record(act, i, LOAD_A, 0, 1)
                load_b = record(act, i, LOAD_B, 0, 1)
                for flag, off_field, t0 in ((load_a, NEXT_OFF_A, 0), (load_b, NEXT_OFF_B, HALF)):
                    with act.If(flag > 0):
                        count8 = record(act, i, NEXT8, 2 * KT, KT * NA)
                        off = record(act, i, off_field, 0, (RING - HALF) * UNIT)
                        for t in range(t0, t0 + HALF):
                            done = KT * (i - 1) + t + HALF + 1 if t0 == 0 else KT * i + t - HALF + 1
                            act.wait_ge(s("steps"), BEFORE3 + done)
                            adapter_hi(None, t, ring[:, bass.ds(off + (t - t0) * UNIT, D)], count8)

            def step(i):
                if i + 1 < SURE:
                    slot_hi(i + 1)
                elif i + 1 < SLOTS:
                    with act.If(n_slots > i + 1):
                        slot_hi(i + 1)
                if i:
                    slot_out(i - 1)
                prefetch(i)

            for i in range(SURE):
                step(i)
            for i in range(SURE, SLOTS):
                with act.If(n_slots > i):
                    step(i)
            for i in range(SURE - 1, SLOTS):
                with act.If(n_slots == i + 1):
                    slot_out(i)
            for i in range(SLOTS):
                if i < SURE:
                    act.wait_ge(s(f"stored{i}"), 32)
                else:
                    with act.If(n_slots > i):
                        act.wait_ge(s(f"stored{i}"), 32)

        @block.vector
        def _(dve):
            as_f32 = lambda ap: ap.bitcast(F32)
            dve.wait_ge(s("eye"), 16)
            dve.wait_ge(s("w1"), 16)
            v = w1_s.rearrange("p (c n) -> p c n", n=T)
            dve.tensor_tensor(v, v, eye[0:T, 0:T].unsqueeze(1).to_broadcast([T, NC_, T]), ALU.add).then_inc(s("w1i"), 1)

            def add_eye(dst):
                dve.tensor_tensor(dst, dst, eye[:, :], ALU.add).then_inc(s("w_eye"), 1)

            def w_eye(u):
                if w_diagonals(u):
                    wait_raw(dve, ("w", u))
                q, h = w_unit(u)
                for k in w_diagonals(u):
                    col = (k - HALF * h) * 256 + (k - 2 * q) * P
                    add_eye(raw[:, raw_of[("w", u)] % RAW, col:col + P])

            def w_lo(u):
                dve.wait_ge(s("w_hi"), u + 1)
                dve.tensor_tensor(w_dst(u, 1), raw_tile(("w", u)).rearrange("p (k o) -> p k o", k=HALF),
                                  as_f32(w_dst(u, 0)), ALU.subtract).then_inc(s("w_lo"), 1)

            def w_pair(u):
                w_eye(u)
                w_eye(u + 1)
                w_lo(u)
                w_lo(u + 1)

            def a_lo(c, k):
                dve.wait_ge(s("x_hi"), KT * c + k + 1)
                dve.tensor_tensor(aT[:, k, 1, :], xT[:, k, CT * c:CT * (c + 1)], as_f32(aT[:, k, 0, :]), ALU.subtract)\
                   .then_inc(s("x_lo"), 1)

            def lora_lo(b):
                dve.wait_ge(s("a_hi"), b + 1)
                v = a_sel[:, b % CB, 0:KT * 2 * R].rearrange("p (k t r) -> p k t r", t=2, r=R)
                dve.tensor_tensor(v[:, :, 1, :], a_raw[:, b % 2, :].rearrange("p (k r) -> p k r", r=R),
                                  as_f32(v[:, :, 0, :]), ALU.subtract).then_inc(s("a_lo"), 1)

            def low_parts(c):
                v = ps_low[:, :, :].rearrange("p a (b t n) -> p (a b) t n", t=2, n=T)
                f = low_f[:, :].rearrange("p (b n) -> p b n", n=T)
                dve.wait_ge(s("low_t"), c + 1)
                dve.tensor_tensor(f, v[:, :, 0, :], f, ALU.add).then_inc(s("low_f"), 1)
                dve.wait_ge(s("low_hi"), c + 1)
                dve.tensor_tensor(low_s[T:P, :], low_f[0:T, :], as_f32(low_s[0:T, :]), ALU.subtract).then_inc(s("low_lo"), 1)

            def make_plan():
                count = [0]

                def do(ins):
                    count[0] += 1
                    ins.then_inc(s("chain"), 1)
                    dve.wait_ge(s("chain"), count[0])

                used = [C_SIZE]

                def cells(n):
                    used[0] += n
                    assert used[0] <= D
                    return small[:, used[0] - n:used[0]]

                def rows(ap, n, m):
                    return ap.unsqueeze(1).to_broadcast([1, n, m])

                def cols(ap, n, m):
                    return ap.unsqueeze(2).to_broadcast([1, n, m])

                def grid(i, n, m):
                    return tmp[i][:, 0:n * m].rearrange("o (n m) -> o n m", m=m)

                def tt(dst, a, b, op):
                    do(dve.tensor_tensor(dst, a, b, op))

                def ts(dst, a, k1, op1, k2=None, op2=None):
                    do(dve.tensor_scalar(dst, a, k1, k2, op1, op2) if op2 is not None else dve.tensor_scalar(dst, a, k1, None, op1))

                def total(dst, src):
                    do(dve.reduce_sum(dst, src, AX.X))

                def weighted(dst, g, weights, n, m, spare=1):
                    tt(grid(spare, n, m), g, weights, ALU.mult)
                    total(dst, grid(spare, n, m))

                e, slot, bat = small[:, C_E:C_E + NA], small[:, C_S:C_S + SLOTS], small[:, C_B:C_B + B]
                below = small[:, C_LT8:C_LT8 + NA * NA].rearrange("o (n m) -> o n m", m=NA)
                dve.wait_ge(s("consts"), 32)
                dve.wait_ge(s("toks"), 48)
                a = cells(B)
                do(dve.tensor_copy(a, toks[0:1, 2, :]))
                cnt, half, occurs = cells(NA), cells(NA), cells(NA)
                tt(grid(0, NA, B), cols(e, NA, B), rows(a, NA, B), ALU.is_equal)
                total(cnt, grid(0, NA, B))
                whole = cells(NA).bitcast(I32)
                ts(whole, cnt, 1.0, ALU.add)
                ts(whole, whole, 1, ALU.logical_shift_right)
                do(dve.tensor_copy(half, whole))
                ts(occurs, cnt, 1.0, ALU.min)
                first, order, last = cells(NA), cells(NA), cells(NA)
                weighted(first, below, rows(half, NA, NA), NA, NA)
                weighted(order, below, rows(occurs, NA, NA), NA, NA)
                tt(last, first, half, ALU.add)
                ts(last, last, -1.0, ALU.add)
                place, rank = cells(B), cells(B)
                tt(grid(0, B, B), cols(a, B, B), rows(a, B, B), ALU.is_equal)
                weighted(rank, grid(0, B, B), before.rearrange("o (n m) -> o n m", m=B), B, B)
                tt(grid(0, B, NA), cols(a, B, NA), rows(e, B, NA), ALU.is_equal)
                weighted(place, grid(0, B, NA), rows(first, B, NA), B, NA)
                ts(place, place, 2.0, ALU.mult)
                tt(place, place, rank, ALU.add)
                S = SLOTS
                twice, b0, b1, there, mine = cells(S), cells(S), cells(S), cells(S), cells(S)
                ts(twice, slot, 2.0, ALU.mult)
                tt(grid(0, S, B), cols(twice, S, B), rows(place, S, B), ALU.is_equal)
                weighted(b0, grid(0, S, B), rows(bat, S, B), S, B)
                weighted(mine, grid(0, S, B), rows(a, S, B), S, B)
                ts(twice, twice, 1.0, ALU.add)
                tt(grid(0, S, B), cols(twice, S, B), rows(place, S, B), ALU.is_equal)
                total(there, grid(0, S, B))
                weighted(b1, grid(0, S, B), rows(bat, S, B), S, B)
                row1, spare_row = cells(S), cells(S)
                ts(spare_row, slot, float(B), ALU.add)
                tt(there, there, spare_row, ALU.mult)
                tt(row1, b1, spare_row, ALU.add)
                tt(row1, row1, there, ALU.subtract)
                nth, lo, hi = cells(S), cells(S), cells(S)
                tt(grid(0, S, NA), cols(mine, S, NA), rows(e, S, NA), ALU.is_equal)
                weighted(nth, grid(0, S, NA), rows(order, S, NA), S, NA)
                weighted(lo, grid(0, S, NA), rows(first, S, NA), S, NA)
                weighted(hi, grid(0, S, NA), rows(last, S, NA), S, NA)
                n_slots, n_active = cells(1), cells(1)
                total(n_slots, half)
                total(n_active, occurs)
                more = cells(S)
                ts(more, nth, 1.0, ALU.add)
                tt(more, more, n_active.to_broadcast([1, S]), ALU.is_lt)
                tt(lo, lo, slot, ALU.is_equal)
                tt(lo, lo, more, ALU.mult)
                tt(hi, hi, slot, ALU.is_equal)
                tt(hi, hi, more, ALU.mult)
                rec = plan[:, HEAD:].rearrange("o (s f) -> o s f", f=FIELDS)

                def put(field, src, k1, k2=0.0):
                    do(dve.tensor_scalar(rec[:, :, field], src, float(k1), float(k2), ALU.mult, ALU.add))

                put(TOK0, b0, T)
                put(TOK1, b1, T)
                put(ROW0, b0, 1)
                put(ROW1, row1, 1)
                put(LOAD_A, lo, 1)
                put(LOAD_B, hi, 1)
                put(THIS8, nth, KT, KT)
                put(NEXT8, nth, KT, 2 * KT)
                at3, wraps = cells(S), cells(S)
                for field, ahead in ((OFF_A, 0), (NEXT_OFF_A, 1), (OFF_B, 2)):
                    ts(at3, nth, float(ahead), ALU.add)
                    for m in (3, 6, 9):
                        ts(wraps, nth, float(m - ahead), ALU.is_ge, -3.0, ALU.mult)
                        tt(at3, at3, wraps, ALU.add)
                    put(field, at3, -HALF * UNIT, KT * UNIT)
                    if field == OFF_A:
                        put(NEXT_OFF_B, at3, -HALF * UNIT, KT * UNIT)
                tt(grid(0, NA, NA), cols(e, NA, NA), rows(order, NA, NA), ALU.is_equal)
                tt(grid(0, NA, NA), grid(0, NA, NA), rows(occurs, NA, NA), ALU.mult)
                ids = cells(NA)
                weighted(ids, grid(0, NA, NA), rows(e, NA, NA), NA, NA)
                do(dve.tensor_copy(plan[:, ADAPTER:ADAPTER + NA], ids))
                do(dve.tensor_copy(plan[:, N_SLOTS:N_SLOTS + 1], n_slots))
                dve.tensor_copy(plan[:, N_ACTIVE:N_ACTIVE + 1], n_active).then_inc(s("plan"), 1)

            w_eye(0)
            w_eye(1)
            w_lo(0)
            w_lo(1)
            for k in range(KT):
                a_lo(0, k)
            for b in range(CB):
                lora_lo(b)
            w_pair(2)
            dve.wait_ge(s("b_hi"), 1)
            dve.scalar_tensor_tensor(b_lo[:, :], b_raw, 0.5, as_f32(b_hi[:, :]), ALU.mult, ALU.subtract).then_inc(s("b_lo"), 1)

            def adapter_lo(t, hi_ap, lo_ap, count8):
                dve.wait_ge(s("w_hi"), count8 + (t + 1))
                dve.tensor_tensor(lo_ap, raw[:, t % RAW, :], as_f32(hi_ap), ALU.subtract).then_inc(s("w_lo"), 1)

            raw_uses = len(raw_seq) // RAW

            def adapter_half(t0, count8, count32, unit_of):
                for t in range(t0, t0 + HALF + 1):
                    if t < t0 + HALF:
                        dve.wait_ge(s(f"raw{t % RAW}"), count32 + 16 * (raw_uses - 2 + t // RAW + 1))
                        add_eye(raw[:, t % RAW, P * t:P * (t + 1)])
                    if t > t0:
                        adapter_lo(t - 1, unit_of(t - 1, 0), unit_of(t - 1, 1), count8)

            for c in range(CH):
                low_parts(c)
                if c == 0:
                    w_pair(4)
                    w_pair(6)
                    make_plan()
                if c + 1 < CH:
                    for b in range(CB * (c + 1), CB * (c + 2)):
                        lora_lo(b)
                    for k in range(KT):
                        a_lo(c + 1, k)

            adapter_half(0, KT, 4 * KT, lambda t, part: unit(KT + t, part))
            adapter_half(HALF, KT, 4 * KT, lambda t, part: unit(t - HALF, part))

            def slot_lo(i):
                for h in range(2):
                    dve.wait_ge(s("s_hi"), 2 * i + h + 1)
                    tok = record(dve, i, TOK0 + h, 0, (B - 1) * T)
                    col = (i % 4) * P + h * T
                    ins = dve.tensor_tensor(aT[:, :, 1, col:col + T], xT[:, :, bass.ds(tok, T)],
                                            as_f32(aT[:, :, 0, col:col + T]), ALU.subtract)
                ins.then_inc(s("s_lo"), 1)

            n_slots = head(dve, N_SLOTS, SURE, SLOTS)
            slot_lo(0)

            def step(i):
                if i + 1 < SURE:
                    slot_lo(i + 1)
                elif i + 1 < SLOTS:
                    with dve.If(n_slots > i + 1):
                        slot_lo(i + 1)
                load_a = record(dve, i, LOAD_A, 0, 1)
                load_b = record(dve, i, LOAD_B, 0, 1)
                for flag, off_field, t0 in ((load_a, NEXT_OFF_A, 0), (load_b, NEXT_OFF_B, HALF)):
                    with dve.If(flag > 0):
                        count8 = record(dve, i, NEXT8, 2 * KT, KT * NA)
                        off = record(dve, i, off_field, 0, (RING - HALF) * UNIT)
                        adapter_half(t0, count8, count8 * 4,
                                     lambda t, part: ring[:, bass.ds(off + (t - t0) * UNIT + part * D, D)])

            for i in range(SURE):
                step(i)
            for i in range(SURE, SLOTS):
                with dve.If(n_slots > i):
                    step(i)

        @block.tensor
        def _(pe):
            pe.wait_ge(s("w0"), 48)
            pe.wait_ge(s("w1i"), 1)
            for h in range(2):
                cols8 = w1_s[:, 512 * h:512 * (h + 1)]
                pe.matmul(ps_mix[0][:, h, :], eye2[:, :], cols8, start=True, stop=False)
                for c in range(8):
                    last = pe.matmul(ps_mix[0][:, h, T * c:T * (c + 1)], w0_s[h][:, P * c:P * (c + 1)],
                                     cols8[:, T * c:T * (c + 1)], start=False, stop=(c == 7))
            last.then_inc(s("mm"), 1)

            def mix(p):
                wait_raw(pe, ("x", p))
                pe.wait_ge(s("bd"), 2 * (p + 1))
                if p >= 2:
                    pe.wait_ge(s("x2"), p - 1)
                src = raw_tile(("x", p))
                for k in range(KT):
                    last = pe.matmul(ps_mix[p % 2][:, k // 4, P * (k % 4):P * (k % 4 + 1)], src[:, P * k:P * (k + 1)],
                                     mix_bd[:, p % (2 * CP), :], start=True, stop=True)
                last.then_inc(s("mixed"), 1)

            def main(c, o, start, stop):
                dst = ps_l2[:, o % 2, :]
                if KT * c + o >= 2 and start:
                    pe.wait_ge(s("x3"), KT * c + o - 1)
                for k in range(KT):
                    if c == 0 and o % 2 == 0 and k % HALF == 0:
                        pe.wait_ge(s("w_lo"), 2 * (o // 2) + k // HALF + 1)
                    if o == 0:
                        pe.wait_ge(s("x_lo"), KT * c + k + 1)
                    cs = slice(P * o, P * (o + 1))
                    pe.matmul(dst, unit(k, 0)[:, cs], aT[:, k, 0, :], start=start and k == 0, stop=False)
                    pe.matmul(dst, unit(k, 0)[:, cs], aT[:, k, 1, :], start=False, stop=False)
                    last = pe.matmul(dst, unit(k, 1)[:, cs], aT[:, k, 0, :], start=False, stop=stop and k == KT - 1)
                    if o == KT - 1:
                        last.then_inc(s("steps"), 1)
                return last

            def low(c):
                if c:
                    pe.wait_ge(s("low_f"), c)
                for b in range(CB):
                    pe.wait_ge(s("a_lo"), CB * c + b + 1)
                    for k in range(KT):
                        last = pe.matmul(ps_low[:, b // 4, P * (b % 4):P * (b % 4 + 1)],
                                         a_sel[:, b, 2 * R * k:2 * R * k + P], aT[:, k, :, T * b:T * (b + 1)],
                                         start=(k == 0), stop=(k == KT - 1))
                last.then_inc(s("low"), 1)

            def delta(c, o, start, stop):
                dst = ps_l2[:, o % 2, :]
                if start:
                    pe.wait_ge(s("x3"), KT * c + o - 1)
                cs = slice(P * o, P * (o + 1))
                pe.matmul(dst, b_hi[:, cs], low_s[:, :], start=start, stop=False)
                return pe.matmul(dst, b_lo[:, cs], low_s[:, :], start=False, stop=stop)

            for p in range(CP):
                mix(p)
            for c in range(CH):
                main(c, 0, True, False)
                low(c)
                main(c, 1, True, False)
                pe.wait_ge(s("low_lo"), c + 1)
                pe.wait_ge(s("b_lo"), 1)
                for o in range(2):
                    delta(c, o, False, True).then_inc(s("l2"), 1)
                for o in range(2, KT):
                    last = delta(c, o, True, False)
                    if c == CH - 1 and o == KT - 1:
                        last.then_inc(s("delta"), 1)
                    last = main(c, o, False, True)
                    if o < KT - 1:
                        last.then_inc(s("l2"), 1)
                    if c + 1 < CH and o - 2 < CP:
                        mix(CP * (c + 1) + o - 2)

            def slot(i):
                count8 = record(pe, i, THIS8, KT, KT * NA)
                offs = [record(pe, i, f, 0, (RING - HALF) * UNIT) for f in (OFF_A, OFF_B)]
                pe.wait_ge(s("s_lo"), i + 1)
                if i >= 4:
                    pe.wait_ge(s("staged"), i - 3)
                for k in range(KT):
                    pe.wait_ge(s("w_lo"), count8 + (k + 1))
                    off = offs[k // HALF] + (k % HALF) * UNIT
                    for m, part in ((0, 0), (0, 1), (1, 0)):
                        for n in range(2):
                            last = pe.matmul(ps[i % 4][:, n, :], aT[:, k, m, P * (i % 4):P * (i % 4 + 1)],
                                             ring[:, bass.ds(off + (part * D + n * 512), 512)],
                                             start=(k == 0 and m == 0 and part == 0),
                                             stop=(k == KT - 1 and m == 1))
                    last.then_inc(s("steps"), 1)

            pe.wait_ge(s("plan"), 1)
            slot_steps(pe, slot)


_OUT = (B + SLOTS, T, D)


def kernel(x, itok_B_0_15, itok_B_0_2, itok_B_3_7, L0_cond_weights, L1_cond_weights, L2_cond_W,
           L2_cond_lora_A, L2_cond_lora_B_w, L3_cond_weight):
    import concourse.bacc as bacc
    from concourse.bass_utils import run_bass_kernel_spmd

    lay = np.ascontiguousarray
    small, before, eye, eye2 = constants()
    w0 = np.asarray(L0_cond_weights).transpose(2, 0, 1)
    w1 = np.asarray(L1_cond_weights).transpose(1, 0, 2)
    la = np.asarray(L2_cond_lora_A).reshape(NL, KT, P, R).transpose(0, 2, 1, 3)
    lb = np.asarray(L2_cond_lora_B_w).transpose(1, 0)
    arrays = {
        "x": lay(x),
        "cond": lay(np.asarray(itok_B_0_15).reshape(1, B)),
        "labeler": lay(np.asarray(itok_B_0_2).reshape(1, B)),
        "adapter": lay(np.asarray(itok_B_3_7).reshape(1, B)),
        "w0t": lay(np.concatenate([w0[:, :, None, :]] * 2, axis=2).reshape(T, 2, D)),
        "w1": lay(w1.reshape(T, NC_ * T)),
        "wt": lay(np.asarray(L2_cond_W).transpose(1, 0)),
        "lora_a": lay(la.reshape(NL, P, KT * R)),
        "lora_b": lay(np.concatenate([lb] * (P // R), axis=0)),
        "w3t": lay(np.asarray(L3_cond_weight).transpose(0, 2, 1)),
        "small_c": small, "before_c": before, "eye_c": eye, "eye2_c": eye2,
    }
    nc = bacc.Bacc("TRN2", target_bir_lowering=False, num_devices=1, dynamic_dma_scratch_size=1024)
    args = {n: nc.dram_tensor(n, a.shape, mybir.dt.from_np(a.dtype), kind="ExternalInput").ap() for n, a in arrays.items()}
    args["out"] = nc.dram_tensor("out", _OUT, F32, kind="ExternalOutput").ap()
    build(nc, **args)
    result = run_bass_kernel_spmd(nc, [arrays], core_ids=[0]).results[0]["out"]
    return result[0:B]
```

```python
import numpy as np
import concourse.bass as bass
from concourse import mybir

F32 = mybir.dt.float32
F32R = mybir.dt.float32r
I32 = mybir.dt.int32
ALU = mybir.AluOpType
ACT = mybir.ActivationFunctionType
AX = mybir.AxisListType

P = 128
B, T, D = 32, 64, 1024
NC_, NL, R, NA = 16, 5, 32, 8
KT = D // P
PAIRS = B // 2
CH = 4
CT = B * T // CH
CB = B // CH
CP = PAIRS // CH
SLOTS = B // 2 + NA // 2
SURE = B // 2
RAW = 4
RING = 12
UNIT = 2 * D
HALF = KT // 2
FIRST = "first"
PLAN_STEPS = 8
WARM = 14
W_AFTER = {0: 0, 3: 1}
EYES_AHEAD = 3
KEEP_WARM = 5

(TOK0, TOK1, ROW0, ROW1, LOAD_A, LOAD_B, NEXT_OFF_A, NEXT_OFF_B, THIS, OFF_A, OFF_B) = range(11)
FIELDS = 11
N_SLOTS, N_ACTIVE, ADAPTER = 0, 1, 2
HEAD = 16
C_E, C_S, C_B, C_LT8 = 0, NA, NA + SLOTS, NA + SLOTS + B
C_SIZE = C_LT8 + NA * NA


def constants():
    small = np.zeros((1, C_SIZE), np.float32)
    small[0, C_E:C_E + NA] = np.arange(NA)
    small[0, C_S:C_S + SLOTS] = np.arange(SLOTS)
    small[0, C_B:C_B + B] = np.arange(B)
    small[0, C_LT8:] = np.tril(np.ones((NA, NA), np.float32), -1).ravel()
    before = np.tril(np.ones((B, B), np.float32), -1).reshape(1, B * B)
    eye = np.eye(P, dtype=np.float32)
    eye2 = np.concatenate([np.eye(T, dtype=np.float32)] * 2, axis=1)
    eyes = np.concatenate([eye, np.concatenate([eye2, np.zeros((P - T, P), np.float32)])], axis=1)
    return small, before, eyes


def build(nc, x, indices, w0t, w1, wt, lora_a, lora_b, w3t, small_c, before_c, eyes_c, out):
    at = [1152]

    def sb(name, shape, dtype, offset=None):
        size = 4 * int(np.prod(shape[1:]))
        if offset is None:
            offset = at[0]
            at[0] += (size + 31) // 32 * 32
        return nc.alloc_sbuf_tensor_at(name, shape, dtype, offset=offset)

    xT_at = at[0]
    xT = sb("xT", [P, KT, B * T], F32)
    aT_at = at[0]
    aT = sb("aT", [P, KT, 2, CT], F32R)
    ring_at = at[0]
    ring = sb("ring", [P, RING * UNIT], F32R)
    raw = sb("raw", [P, RAW, D], F32)
    eyes = sb("eyes", [P, 2 * P], F32)
    eye, eye2 = eyes[:, 0:P], eyes[0:T, P:2 * P]
    plan = sb("plan", [1, HEAD + SLOTS * FIELDS], I32)
    toks = sb("toks", [1, 3, B], I32)
    stage_at = at[0]
    stage = sb("stage", [P, 2, D], F32)
    mix_tab = sb("mix_tab", [P, NC_ * T], F32, offset=stage_at)
    mix_bd = sb("mix_bd", [P, 2 * CP, P], F32, offset=stage_at + 4 * NC_ * T)
    s_at = ring_at + 4 * UNIT * KT
    a_sel = sb("a_sel", [P, CP, KT, 2, 2, R], F32R, offset=s_at)
    s_at += 4 * CP * KT * 4 * R
    b_split = sb("b_split", [P, D], F32R, offset=s_at)
    s_at += 4 * D
    low_split = sb("low_split", [P, CT], F32R, offset=s_at)
    low = sb("low", [P, CT], F32, offset=s_at + 4 * CT)
    a_raw = sb("a_raw", [P, 2, KT * R], F32, offset=s_at + 8 * CT)
    assert s_at + 8 * CT + 8 * KT * R <= ring_at + 4 * UNIT * RING
    late = lambda k: xT[:, k, 2 * CT:4 * CT]
    small = xT[0:1, 0, 2 * CT:4 * CT]
    before = xT[0:1, 1, 2 * CT:4 * CT]
    w1_s = xT[0:T, 2, 2 * CT:4 * CT]
    w0_s = [xT[0:T, 3 + h, 2 * CT:4 * CT] for h in range(2)]
    b_raw = late(5)
    tmp = [xT[0:1, 6 + i, 2 * CT:4 * CT] for i in range(2)]
    half_w = lambda ap: ap.rearrange("p (k o) -> p k o", k=HALF)
    w_early = [half_w(late(6)), half_w(late(7)), xT[:, 0:HALF, CT + 256:2 * CT], xT[:, HALF:KT, CT + 256:2 * CT],
               half_w(late(3)), half_w(late(4))]
    EARLY = len(w_early)

    def unit(g, part):
        return ring[:, g * UNIT + part * D:g * UNIT + (part + 1) * D]

    ps = [nc.alloc_psum_tensor(f"ps{i}", [P, 2, 512], F32) for i in range(4)]
    ps_mix, ps_low = ps[0:2], ps[2]

    def l2_place(c, o):
        return (7 * c + o - (o > 2)) % 2 if o != 2 else 2

    def ps_l2(c, o):
        return ps_mix[1][:, 1, :] if o == 2 else ps[3][:, l2_place(c, o), :]

    def l2_before(c, o):
        n = [KT * d + q + 1 for d in range(CH) for q in range(KT)
             if (d, q) < (c, o) and l2_place(d, q) == l2_place(c, o)]
        return n[-1] if n else 0

    def x2_of(c, k):
        return ps_mix[k // 2 % 2][:, k % 2, :] if c == 0 else xT[:, k, CT * c:CT * (c + 1)]

    sem = {}

    def s(name):
        if name not in sem:
            sem[name] = nc.alloc_semaphore(name)
        return sem[name]

    raw_seq = [("x", p) for p in range(CP)] + [("w", u) for u in range(EARLY, KT)] + [("x", p) for p in range(CP, PAIRS)]
    raw_of = {e: n for n, e in enumerate(raw_seq)}
    RING_USES = len(raw_seq)

    aT_raw = sb("aT_raw", [P, KT, 2, CT], F32, offset=aT_at)

    def adapter_raw(t, first):
        if first or t < HALF:
            return raw[:, (RING_USES + t) % RAW, :].rearrange("p (q n) -> p q n", q=4)
        return aT_raw[:, 2 * (t - HALF):2 * (t - HALF) + 2, :, CT // 2:].rearrange("p k m n -> p (k m) n")

    def adapter_loaded(t, first, n):
        if first or t < HALF:
            slot = (RING_USES + t) % RAW
            before_ = (RING_USES + t) // RAW
            if first:
                return s(f"raw{slot}"), 16 * (before_ + 1)
            total_first = len([u for u in range(RING_USES + KT) if u % RAW == slot])
            return s(f"raw{slot}"), n * 16 + 16 * total_first
        return s(f"a_hold{t}"), n * 16

    def as4(ap):
        return ap.rearrange("p (q n) -> p q n", q=4)

    def wait_raw(eng, entry):
        n = raw_of[entry]
        eng.wait_ge(s(f"raw{n % RAW}"), 16 * (n // RAW + 1))

    def raw_tile(entry):
        return raw[:, raw_of[entry] % RAW, :]

    def w_unit(u):
        return u // 2, u % 2

    def w_raw(u):
        return w_early[u] if u < EARLY else raw_tile(("w", u)).rearrange("p (k o) -> p k o", k=HALF)

    def wait_w(eng, u):
        if u < EARLY:
            eng.wait_ge(s(f"w_raw{u}"), 16)
        else:
            wait_raw(eng, ("w", u))

    def low_parts_of(part):
        return ps_low[:, :, :].rearrange("p a (j t n) -> p (a j) t n", t=2, n=P)[:, :, part, :]

    def of_batch(ap, h):
        return ap.rearrange("p (j h n) -> p j h n", h=2, n=T)[:, :, h, :]

    def a_raw_of(b):
        if b < CB:
            return xT[:, b, CT:CT + KT * R], s(f"a_raw{b}"), 16
        return a_raw[:, b % 2, :], s(f"a_ring{b % 2}"), 16 * ((b - CB) // 2 + 1)

    def w_diagonals(u):
        q, h = w_unit(u)
        return [k for k in (2 * q, 2 * q + 1) if k // HALF == h]

    def w_dst(u, part):
        q, h = w_unit(u)
        v = ring[:, :].rearrange("p (g t n) -> p g t n", t=2, n=D)
        return v[:, HALF * h:HALF * (h + 1), part, 256 * q:256 * (q + 1)]

    def record(eng, slot, field, lo, hi):
        i = HEAD + slot * FIELDS + field
        return eng.value_load(plan[0:1, i:i + 1], min_val=lo, max_val=hi)

    def head(eng, i, lo, hi):
        return eng.value_load(plan[0:1, i:i + 1], min_val=lo, max_val=hi)

    def slot_steps(eng, body, last=SLOTS):
        n = head(eng, N_SLOTS, SURE, SLOTS)
        for i in range(last):
            if i < SURE:
                body(i)
            else:
                with eng.If(n > i):
                    body(i)

    BEFORE3 = 8 * CH

    with nc.Block() as block:

        @block.sync
        def _(sp):
            xp = x.rearrange("(q two) t d -> q (two t) d", two=2)
            wv = wt.rearrange("(k p) o -> p k o", p=P)

            def raw_free(n):
                if n >= RAW:
                    kind, i = raw_seq[n - RAW] if n - RAW < len(raw_seq) else ("a", n - RAW - len(raw_seq))
                    if kind == "x" and i < CP:
                        sp.wait_ge(s("mixed0"), KT)
                    elif kind == "x":
                        sp.wait_ge(s("mixed"), i - CP + 1)
                    else:
                        sp.wait_ge(s("w_lo"), i + 1 if kind == "w" else KT + i + 1)

            def load_raw(entry):
                n = raw_of[entry]
                raw_free(n)
                kind, i = entry
                dst, src = (raw[:, n % RAW, :], xp[i, :, :]) if kind == "x" else (w_raw(i), w_src(i))
                sp.dma_start(dst, src).then_inc(s(f"raw{n % RAW}"), 16)

            def w_src(u):
                q, h = w_unit(u)
                return wv[:, HALF * h:HALF * (h + 1), 256 * q:256 * (q + 1)]

            def load_a(b):
                if b >= CB + 2:
                    sp.wait_ge(s("a_lo"), b - 1)
                dst, loaded, _ = a_raw_of(b)
                l = sp.value_load(toks[0:1, 1, b:b + 1], min_val=0, max_val=NL - 1)
                sp.dma_start(dst, lora_a[bass.ds(l, 1), :, :].rearrange("a p n -> p (a n)")).then_inc(loaded, 16)

            sp.dma_start(w1_s, w1).then_inc(s("w1"), 16)
            for h in range(2):
                sp.dma_start(w0_s[h], w0t[:, h, :]).then_inc(s(f"w0_{h}"), 16)
            for e in raw_seq[0:CP]:
                load_raw(e)

            def load_w(u):
                sp.dma_start(w_early[u], w_src(u)).then_inc(s(f"w_raw{u}"), 16)

            load_w(0)
            load_w(1)
            sp.wait_ge(s("toks"), 16)
            for b in range(CB):
                load_a(b)
            load_w(2)
            load_w(3)
            sp.dma_start(b_raw, lora_b).then_inc(s("b_raw"), 16)
            sp.wait_ge(s("mm"), 2)
            load_w(4)
            load_w(5)
            sp.dma_start(small[:, 0:C_SIZE], small_c).then_inc(s("consts"), 16)
            sp.dma_start(before, before_c).then_inc(s("consts"), 16)
            for e in raw_seq[CP:CP + KT - EARLY]:
                load_raw(e)
            for c in range(1, CH):
                for j in range(CP):
                    load_raw(("x", c * CP + j))
                    load_a(c * CB + 2 * j)
                    load_a(c * CB + 2 * j + 1)
            sp.wait_ge(s("plan"), 1)
            n_active = head(sp, N_ACTIVE, 1, NA)
            for k in range(NA):
                def load_adapter(k=k):
                    e = head(sp, ADAPTER + k, 0, NA - 1)
                    for t in range(KT):
                        if k == 0:
                            raw_free(RING_USES + t)
                        else:
                            if t < HALF:
                                last = KT * k + max(u for u in range(KT) if (u - t) % RAW == 0 and (k == 1 or u < HALF))
                            else:
                                last = KT * k + t
                            if k > 1 or t < HALF:
                                sp.wait_ge(s("w_lo"), last + 1)
                            elif t == HALF:
                                sp.wait_ge(s("steps"), BEFORE3)
                        src = w3t[bass.ds(e, 1), t * P:(t + 1) * P, :].rearrange("a p (q n) -> p (a q) n", q=4)
                        loaded, _ = adapter_loaded(t, k == 0, k)
                        sp.dma_start(adapter_raw(t, k == 0), src).then_inc(loaded, 16)
                if k == 0:
                    load_adapter()
                else:
                    with sp.If(n_active > k):
                        load_adapter()

        @block.gpsimd
        def _(pool):
            pool.memset(mix_bd[:, 0:1, :], 0.0).then_inc(s("zeroed"), 1)
            pool.memset(mix_bd[:, 1:2 * CP, :], 0.0).then_inc(s("zeroed"), 1)
            pool.wait_ge(s("toks"), 16)

            def condition(b):
                return pool.value_load(toks[0:1, 0, b:b + 1], min_val=0, max_val=NC_ - 1)

            ahead = [condition(b) for b in range(CB, 2 * CB)]
            pool.wait_ge(s("zeroed"), 2)
            pool.wait_ge(s("mix_tab"), 2)
            for p in range(CP, PAIRS):
                if 2 * CP <= p < 3 * CP:
                    pool.wait_ge(s("mixed0"), KT)
                elif p >= 3 * CP:
                    pool.wait_ge(s("mixed"), p - 3 * CP + 1)
                for h in range(2):
                    b = 2 * p + h
                    c = ahead[b - CB] if b < 2 * CB else condition(b)
                    rows = slice(h * T, (h + 1) * T)
                    pool.tensor_copy(mix_bd[rows, p % (2 * CP), h * T:(h + 1) * T],
                                     mix_tab[rows, bass.ds(c * T, T)]).then_inc(s("bd"), 1)

        @block.scalar
        def _(act):
            act.dma_start(eyes[:, :], eyes_c).then_inc(s("eye"), 16)
            act.dma_start(toks[:, :, :], indices).then_inc(s("toks"), 16)

            def mix_out(p):
                act.wait_ge(s("mixed"), p - CP + 1)
                if p == CP:
                    act.wait_ge(s("w_lo"), EARLY)
                    act.wait_ge(s("a_lo"), CB)
                if p == 2 * CP:
                    act.wait_ge(s("plan"), 1)
                    act.wait_ge(s("b_split"), 2)
                act.activation(xT[:, :, P * p:P * (p + 1)],
                               ps_mix[p % 2][:, :, :].rearrange("p a (k n) -> p (a k) n", n=P), ACT.Copy)\
                   .then_inc(s("x2"), 1)

            def w_hi(u):
                if w_diagonals(u):
                    act.wait_ge(s("w_eye"), sum(len(w_diagonals(v)) for v in range(u + 1)))
                else:
                    wait_w(act, u)
                act.activation(w_dst(u, 0), w_raw(u), ACT.Copy)\
                   .then_inc(s("w_hi"), 1)

            def a_hi(c, k):
                if c:
                    act.wait_ge(s("x2"), CP * c)
                    act.wait_ge(s("steps"), KT * (c - 1) + k + 1)
                else:
                    act.wait_ge(s("mixed0"), k + 1)
                act.activation(aT[:, k, 0, :], x2_of(c, k), ACT.Copy).then_inc(s("x_hi"), 1)

            def lora_hi(b):
                src, loaded, value = a_raw_of(b)
                act.wait_ge(loaded, value)
                act.wait_ge(s("low"), b // CB)
                act.activation(a_sel[:, b % CB // 2, :, b % 2, 0, :],
                               src.rearrange("p (k r) -> p k r", r=R), ACT.Copy).then_inc(s("a_hi"), 1)

            def low_out(c):
                act.wait_ge(s("low"), c + 1)
                act.activation(low[:, :].rearrange("p (j n) -> p j n", n=P), low_parts_of(1), ACT.Copy).then_inc(s("low_cols"), 1)
                act.wait_ge(s("low_sum"), c + 1)
                act.wait_ge(s("steps"), KT * c)
                for h, src, dst, n in ((0, 0, 0, 2), (1, 2, 2, 1), (1, 2, 0, 2), (0, 0, 3, 1), (1, 2, 3, 1)):
                    act.activation(of_batch(low_split[R * dst:R * (dst + n), :], h),
                                   of_batch(low[R * src:R * (src + n), :], h), ACT.Copy).then_inc(s("low_hi"), 1)

            def l2_out(c, o):
                if o < KT - 1:
                    act.wait_ge(s("l2"), (KT - 1) * c + o + 1)
                else:
                    act.wait_ge(s("steps"), KT * (c + 1))
                act.activation(xT[:, o, CT * c:CT * (c + 1)], ps_l2(c, o), ACT.Copy).then_inc(s("x3"), 1)

            for k in range(KT):
                a_hi(0, k)
                if k in W_AFTER:
                    w_hi(W_AFTER[k])
                if k == HALF:
                    act.wait_ge(s("bd"), CB)
                    for h in range(2):
                        act.activation(mix_tab[:, 512 * h:512 * (h + 1)], ps_low[:, h, :], ACT.Copy).then_inc(s("mix_tab"), 1)
            for b in range(CB):
                lora_hi(b)
            w_hi(2)
            w_hi(3)
            act.wait_ge(s("b_raw"), 16)
            act.activation(b_split[:, :], b_raw, ACT.Copy, scale=0.5).then_inc(s("b_split"), 1)
            w_hi(4)
            w_hi(5)

            def adapter_hi(k, t, dst, count8):
                act.wait_ge(s("w_eye"), count8 + (t + 1))
                act.activation(dst, adapter_raw(t, k == 0), ACT.Copy).then_inc(s("w_hi"), 1)

            for c in range(CH):
                low_out(c)
                if c == 0:
                    w_hi(6)
                    w_hi(7)
                l2_out(c, 0)
                l2_out(c, 1)
                for o in range(2, KT - 1):
                    l2_out(c, o)
                    if c + 1 < CH:
                        if o - 2 < CP:
                            mix_out(CP * (c + 1) + o - 2)
                        for b in range(2 * (o - 2), min(2 * (o - 1), CB)):
                            lora_hi(CB * (c + 1) + b)
                    elif o < 4:
                        act.wait_ge(s("low"), CH)
                        adapter_hi(0, o - 2, as4(unit(KT + o - 2, 0)), KT)
                if c + 1 < CH:
                    for k in range(KT):
                        a_hi(c + 1, k)
                else:
                    act.wait_ge(s("delta"), 1)
                    for t in range(2, HALF):
                        adapter_hi(0, t, as4(unit(KT + t, 0)), KT)
                if c + 1 < CH:
                    l2_out(c, KT - 1)

            def slot_hi(i, tiles=(0, KT)):
                toks_ = [record(act, i, TOK0 + h, 0, (B - 1) * T) for h in range(2)]
                ks = slice(*tiles)
                act.wait_ge(s("steps"), BEFORE3 + (KT * (i - 1) if i else tiles[1] - KT))
                for h in range(2):
                    col = (i % 2) * P + h * T
                    act.activation(aT[:, ks, 0, col:col + T], xT[:, ks, bass.ds(toks_[h], T)], ACT.Copy).then_inc(s("s_hi"), 1)

            def slot_out(i):
                rows = [record(act, i, ROW0 + h, 0, B + SLOTS - 1) for h in range(2)]
                act.wait_ge(s("steps"), BEFORE3 + KT * (i + 1))
                if i >= 2:
                    act.wait_ge(s(f"stored{i - 2}"), 32)
                act.activation(stage[:, i % 2, :], ps[i % 4][:, :, :].rearrange("p a n -> p (a n)"), ACT.Copy)\
                   .then_inc(s("staged"), 1)
                act.wait_ge(s("staged"), i + 1)
                for h in range(2):
                    act.dma_start(out[bass.ds(rows[h], 1), :, :].rearrange("a t d -> (a t) d"),
                                  stage[h * T:(h + 1) * T, i % 2, :]).then_inc(s(f"stored{i}"), 16)

            act.wait_ge(s("plan"), 1)
            act.wait_ge(s("x3"), KT * CH - 1)
            slot_hi(0, (0, HALF))
            l2_out(CH - 1, KT - 1)
            act.wait_ge(s("x3"), KT * CH)
            slot_hi(0, (HALF, KT))
            for t in range(HALF, KT):
                adapter_hi(0, t, as4(unit(t - HALF, 0)), KT)
            n_slots = head(act, N_SLOTS, SURE, SLOTS)

            def prefetch(i):
                load_a = record(act, i, LOAD_A, 0, 1)
                load_b = record(act, i, LOAD_B, 0, 1)
                for flag, off_field, t0 in ((load_a, NEXT_OFF_A, 0), (load_b, NEXT_OFF_B, HALF)):
                    with act.If(flag > 0):
                        count8 = (record(act, i, THIS, 1, NA - 1) + 1) * KT
                        off = record(act, i, off_field, 0, (RING - HALF) * UNIT)
                        for t in range(t0, t0 + HALF):
                            done = KT * (i - 1) + t + HALF + 1 if t0 == 0 else KT * i + t - HALF + 1
                            act.wait_ge(s("steps"), BEFORE3 + done)
                            adapter_hi(None, t, as4(ring[:, bass.ds(off + (t - t0) * UNIT, D)]), count8)

            def step(i):
                if i + 1 < SURE:
                    slot_hi(i + 1)
                elif i + 1 < SLOTS:
                    with act.If(n_slots > i + 1):
                        slot_hi(i + 1)
                if i:
                    slot_out(i - 1)
                prefetch(i)

            for i in range(SURE):
                step(i)
            for i in range(SURE, SLOTS):
                with act.If(n_slots > i):
                    step(i)
            for i in range(SURE - 1, SLOTS):
                with act.If(n_slots == i + 1):
                    slot_out(i)
            for i in range(SLOTS):
                if i < SURE:
                    act.wait_ge(s(f"stored{i}"), 32)
                else:
                    with act.If(n_slots > i):
                        act.wait_ge(s(f"stored{i}"), 32)

        @block.vector
        def _(dve):
            as_f32 = lambda ap: ap.bitcast(F32)
            dve.wait_ge(s("eye"), 16)
            dve.wait_ge(s("w1"), 16)
            for h in range(2):
                v = w1_s[:, 512 * h:512 * (h + 1)].rearrange("p (c n) -> p c n", n=T)
                dve.tensor_tensor(v, v, eyes[0:T, 0:T].unsqueeze(1).to_broadcast([T, NC_ // 2, T]), ALU.add)\
                   .then_inc(s("w1i"), 1)

            dve.wait_ge(s("toks"), 16)
            ahead = [dve.value_load(toks[0:1, 0, b:b + 1], min_val=0, max_val=NC_ - 1) for b in range(CB)]
            dve.wait_ge(s("zeroed"), 2)
            dve.wait_ge(s("mm"), 2)
            table = ps_low[:, :, :].rearrange("p a n -> p (a n)")
            for b in range(CB):
                rows = slice(b % 2 * T, (b % 2 + 1) * T)
                dve.tensor_copy(mix_bd[rows, b // 2, b % 2 * T:(b % 2 + 1) * T], table[rows, bass.ds(ahead[b] * T, T)])\
                   .then_inc(s("bd"), 1)

            def add_eye(dst):
                dve.tensor_tensor(dst, dst, eye, ALU.add).then_inc(s("w_eye"), 1)

            def w_eye(u):
                if w_diagonals(u):
                    wait_w(dve, u)
                q, h = w_unit(u)
                for k in w_diagonals(u):
                    add_eye(w_raw(u)[:, k - HALF * h, (k - 2 * q) * P:(k - 2 * q + 1) * P])

            def w_lo(u):
                dve.wait_ge(s("w_hi"), u + 1)
                dve.tensor_tensor(w_dst(u, 1), w_raw(u), as_f32(w_dst(u, 0)), ALU.subtract).then_inc(s("w_lo"), 1)

            def w_pair(u):
                w_eye(u)
                w_eye(u + 1)
                w_lo(u)
                w_lo(u + 1)

            def a_lo(c, k):
                dve.wait_ge(s("x_hi"), KT * c + k + 1)
                dve.tensor_tensor(aT[:, k, 1, :], x2_of(c, k), as_f32(aT[:, k, 0, :]), ALU.subtract)\
                   .then_inc(s("x_lo"), 1)

            def lora_lo(b):
                dve.wait_ge(s("a_hi"), b + 1)
                v = a_sel[:, b % CB // 2, :, b % 2, :, :]
                dve.tensor_tensor(v[:, :, 1, :], a_raw_of(b)[0].rearrange("p (k r) -> p k r", r=R),
                                  as_f32(v[:, :, 0, :]), ALU.subtract).then_inc(s("a_lo"), 1)

            def low_parts(c):
                v = low[:, :].rearrange("p (j n) -> p j n", n=P)
                dve.wait_ge(s("low_cols"), c + 1)
                dve.tensor_tensor(v, low_parts_of(0), v, ALU.add).then_inc(s("low_sum"), 1)
                for h, src in ((0, 0), (1, 2)):
                    dve.wait_ge(s("low_hi"), 5 * c + h + 1)
                    rows = slice(R * src, R * (src + 1))
                    dve.tensor_tensor(of_batch(low_split[2 * R:3 * R, :], h), of_batch(low[rows, :], h),
                                      as_f32(of_batch(low_split[rows, :], h)), ALU.subtract).then_inc(s("low_lo"), 1)

            def make_plan():
                steps = []
                def do(emit, *args):
                    steps.append((emit, args))

                used = [C_SIZE]

                def cells(n):
                    used[0] += n
                    assert used[0] <= D
                    return small[:, used[0] - n:used[0]]

                def rows(ap, n, m):
                    return ap.unsqueeze(1).to_broadcast([1, n, m])

                def cols(ap, n, m):
                    return ap.unsqueeze(2).to_broadcast([1, n, m])

                def grid(i, n, m):
                    return tmp[i][:, 0:n * m].rearrange("o (n m) -> o n m", m=m)

                def tt(dst, a, b, op):
                    do(dve.tensor_tensor, dst, a, b, op)

                def ts(dst, a, k1, op1, k2=None, op2=None):
                    do(dve.tensor_scalar, dst, a, k1, k2, *((op1,) if op2 is None else (op1, op2)))

                def total(dst, src):
                    do(dve.reduce_sum, dst, src, AX.X)

                def weighted(dst, g, weights, n, m, spare=1):
                    tt(grid(spare, n, m), g, weights, ALU.mult)
                    total(dst, grid(spare, n, m))

                e, slot, bat = small[:, C_E:C_E + NA], small[:, C_S:C_S + SLOTS], small[:, C_B:C_B + B]
                below = small[:, C_LT8:C_LT8 + NA * NA].rearrange("o (n m) -> o n m", m=NA)
                a = cells(B)
                do(dve.tensor_copy, a, toks[0:1, 2, :])
                cnt, half, occurs = cells(NA), cells(NA), cells(NA)
                tt(grid(0, NA, B), cols(e, NA, B), rows(a, NA, B), ALU.is_equal)
                total(cnt, grid(0, NA, B))
                whole = cells(NA).bitcast(I32)
                ts(whole, cnt, 1.0, ALU.add)
                ts(whole, whole, 1, ALU.logical_shift_right)
                do(dve.tensor_copy, half, whole)
                ts(occurs, cnt, 1.0, ALU.min)
                first, order, last = cells(NA), cells(NA), cells(NA)
                weighted(first, below, rows(half, NA, NA), NA, NA)
                weighted(order, below, rows(occurs, NA, NA), NA, NA)
                tt(last, first, half, ALU.add)
                ts(last, last, -1.0, ALU.add)
                place, rank = cells(B), cells(B)
                tt(grid(0, B, B), cols(a, B, B), rows(a, B, B), ALU.is_equal)
                weighted(rank, grid(0, B, B), before.rearrange("o (n m) -> o n m", m=B), B, B)
                tt(grid(0, B, NA), cols(a, B, NA), rows(e, B, NA), ALU.is_equal)
                weighted(place, grid(0, B, NA), rows(first, B, NA), B, NA)
                ts(place, place, 2.0, ALU.mult)
                tt(place, place, rank, ALU.add)
                S = SLOTS
                twice, b0, b1, there, mine = cells(S), cells(S), cells(S), cells(S), cells(S)
                ts(twice, slot, 2.0, ALU.mult)
                tt(grid(0, S, B), cols(twice, S, B), rows(place, S, B), ALU.is_equal)
                weighted(b0, grid(0, S, B), rows(bat, S, B), S, B)
                weighted(mine, grid(0, S, B), rows(a, S, B), S, B)
                ts(twice, twice, 1.0, ALU.add)
                tt(grid(0, S, B), cols(twice, S, B), rows(place, S, B), ALU.is_equal)
                total(there, grid(0, S, B))
                weighted(b1, grid(0, S, B), rows(bat, S, B), S, B)
                row1, spare_row = cells(S), cells(S)
                ts(spare_row, slot, float(B), ALU.add)
                tt(there, there, spare_row, ALU.mult)
                tt(row1, b1, spare_row, ALU.add)
                tt(row1, row1, there, ALU.subtract)
                nth, lo, hi = cells(S), cells(S), cells(S)
                tt(grid(0, S, NA), cols(mine, S, NA), rows(e, S, NA), ALU.is_equal)
                weighted(nth, grid(0, S, NA), rows(order, S, NA), S, NA)
                weighted(lo, grid(0, S, NA), rows(first, S, NA), S, NA)
                weighted(hi, grid(0, S, NA), rows(last, S, NA), S, NA)
                n_slots, n_active = cells(1), cells(1)
                total(n_slots, half)
                total(n_active, occurs)
                more = cells(S)
                ts(more, nth, 1.0, ALU.add)
                tt(more, more, n_active.to_broadcast([1, S]), ALU.is_lt)
                tt(lo, lo, slot, ALU.is_equal)
                tt(lo, lo, more, ALU.mult)
                tt(hi, hi, slot, ALU.is_equal)
                tt(hi, hi, more, ALU.mult)
                rec = plan[:, HEAD:].rearrange("o (s f) -> o s f", f=FIELDS)

                def put(field, src, k1, k2=0.0):
                    do(dve.tensor_scalar, rec[:, :, field], src, float(k1), float(k2), ALU.mult, ALU.add)

                put(TOK0, b0, T)
                put(TOK1, b1, T)
                put(ROW0, b0, 1)
                put(ROW1, row1, 1)
                put(LOAD_A, lo, 1)
                put(LOAD_B, hi, 1)
                put(THIS, nth, 1, 1)
                at3, wraps = cells(S), cells(S)
                for field, ahead in ((OFF_A, 0), (NEXT_OFF_A, 1), (OFF_B, 2)):
                    ts(at3, nth, float(ahead), ALU.add)
                    for m in (3, 6, 9):
                        ts(wraps, nth, float(m - ahead), ALU.is_ge, -3.0, ALU.mult)
                        tt(at3, at3, wraps, ALU.add)
                    put(field, at3, -HALF * UNIT, KT * UNIT)
                    if field == OFF_A:
                        put(NEXT_OFF_B, at3, -HALF * UNIT, KT * UNIT)
                tt(grid(0, NA, NA), cols(e, NA, NA), rows(order, NA, NA), ALU.is_equal)
                tt(grid(0, NA, NA), grid(0, NA, NA), rows(occurs, NA, NA), ALU.mult)
                ids = cells(NA)
                weighted(ids, grid(0, NA, NA), rows(e, NA, NA), NA, NA)
                do(dve.tensor_copy, plan[:, ADAPTER:ADAPTER + NA], ids)
                do(dve.tensor_copy, plan[:, N_SLOTS:N_SLOTS + 1], n_slots)
                do(dve.tensor_copy, plan[:, N_ACTIVE:N_ACTIVE + 1], n_active)
                return steps

            def take(steps, done, n):
                for emit, args in steps[done:done + n]:
                    dve.wait_ge(s("chain"), done)
                    done += 1
                    emit(*args).then_inc(s("plan" if done == len(steps) else "chain"), 1)
                return done


            w_eye(0)
            for k in range(KT):
                a_lo(0, k)
                if k in W_AFTER:
                    w_lo(W_AFTER[k])
                if k == 1:
                    w_eye(1)
            for b in range(CB):
                lora_lo(b)
            w_pair(2)
            dve.wait_ge(s("b_split"), 1)
            dve.scalar_tensor_tensor(b_split[3 * R:, :], b_raw[3 * R:, :], 0.5, as_f32(b_split[3 * R:, :]),
                                     ALU.mult, ALU.subtract).then_inc(s("b_split"), 1)
            w_pair(4)

            def adapter_half(t0, n, unit_of):
                first = n is FIRST
                n = 0 if first else n
                for t in range(t0, t0 + HALF + EYES_AHEAD):
                    if t < t0 + HALF:
                        dve.wait_ge(*adapter_loaded(t, first, n))
                        q, col = divmod(P * t, D // 4)
                        add_eye(adapter_raw(t, first)[:, q, col:col + P])
                    u = t - EYES_AHEAD
                    if u >= t0:
                        dve.wait_ge(s("w_hi"), n * KT + (KT + u + 1))
                        dve.tensor_tensor(as4(unit_of(u, 1)), adapter_raw(u, first),
                                          as_f32(as4(unit_of(u, 0))), ALU.subtract).then_inc(s("w_lo"), 1)

            for c in range(CH):
                low_parts(c)
                if c == 1:
                    done = take(steps, done, len(steps))
                if c == 0:
                    w_pair(6)
                    steps, done = make_plan(), 0
                    dve.wait_ge(s("consts"), 32)
                    dve.wait_ge(s("toks"), 16)
                if c + 1 < CH:
                    for b in range(CB * (c + 1), CB * (c + 2)):
                        lora_lo(b)
                        if c == 0:
                            done = take(steps, done, PLAN_STEPS)
                    for k in range(KT):
                        a_lo(c + 1, k)

            adapter_half(0, FIRST, lambda t, part: unit(KT + t, part))

            def slot_lo(i, tiles=(0, KT)):
                toks_ = [record(dve, i, TOK0 + h, 0, (B - 1) * T) for h in range(2)]
                ks = slice(*tiles)
                before_ = 2 * i + 2 if i else 2 * (tiles[0] // HALF)
                for h in range(2):
                    dve.wait_ge(s("s_hi"), before_ + h + 1)
                    col = (i % 2) * P + h * T
                    ins = dve.tensor_tensor(aT[:, ks, 1, col:col + T], xT[:, ks, bass.ds(toks_[h], T)],
                                            as_f32(aT[:, ks, 0, col:col + T]), ALU.subtract)
                ins.then_inc(s("s_lo"), 1)

            slot_lo(0, (0, HALF))
            slot_lo(0, (HALF, KT))
            adapter_half(HALF, FIRST, lambda t, part: unit(t - HALF, part))
            n_slots = head(dve, N_SLOTS, SURE, SLOTS)

            def step(i):
                if i + 1 < SURE:
                    slot_lo(i + 1)
                elif i + 1 < SLOTS:
                    with dve.If(n_slots > i + 1):
                        slot_lo(i + 1)
                load_a = record(dve, i, LOAD_A, 0, 1)
                load_b = record(dve, i, LOAD_B, 0, 1)
                for flag, off_field, t0 in ((load_a, NEXT_OFF_A, 0), (load_b, NEXT_OFF_B, HALF)):
                    with dve.If(flag > 0):
                        n = record(dve, i, THIS, 1, NA - 1)
                        off = record(dve, i, off_field, 0, (RING - HALF) * UNIT)
                        adapter_half(t0, n, lambda t, part: ring[:, bass.ds(off + (t - t0) * UNIT + part * D, D)])

            for i in range(SURE):
                step(i)
            for i in range(SURE, SLOTS):
                with dve.If(n_slots > i):
                    step(i)

        @block.tensor
        def _(pe):
            pe.wait_ge(s("zeroed"), 1)
            for i in range(WARM):
                pe.matmul(ps[3][:, 0, 0:P], mix_bd[:, 0, :], mix_bd[:, 0, :], start=True, stop=True)

            for h in range(2):
                pe.wait_ge(s("w1i"), h + 1)
                pe.wait_ge(s(f"w0_{h}"), 16)
                cols8 = w1_s[:, 512 * h:512 * (h + 1)]
                pe.matmul(ps_low[:, h, :], eye2, cols8, start=True, stop=False)
                for c in range(8):
                    last = pe.matmul(ps_low[:, h, T * c:T * (c + 1)], w0_s[h][:, P * c:P * (c + 1)],
                                     cols8[:, T * c:T * (c + 1)], start=False, stop=(c == 7))
                last.then_inc(s("mm"), 1)

            pe.wait_ge(s("eye"), 16)
            for i in range(KEEP_WARM):
                pe.matmul(ps[3][:, 0, 0:P], eye, eye, start=True, stop=True)

            def mix_tile(p, k, dst):
                return pe.matmul(dst, raw_tile(("x", p))[:, P * k:P * (k + 1)], mix_bd[:, p % (2 * CP), :],
                                 start=True, stop=True)

            def mix0(k):
                if k >= 4:
                    pe.wait_ge(s("x_lo"), k - 3)
                for p in range(CP):
                    if k == 0:
                        wait_raw(pe, ("x", p))
                        pe.wait_ge(s("bd"), 2 * (p + 1))
                    last = mix_tile(p, k, x2_of(0, k)[:, P * p:P * (p + 1)])
                last.then_inc(s("mixed0"), 1)

            def mix(p):
                wait_raw(pe, ("x", p))
                pe.wait_ge(s("bd"), 2 * (p + 1))
                if p >= CP + 2:
                    pe.wait_ge(s("x2"), p - CP - 1)
                if p % 2:
                    pe.wait_ge(s("x3"), KT * (p // CP - 1) + 3)
                for k in range(KT):
                    last = mix_tile(p, k, ps_mix[p % 2][:, k // 4, P * (k % 4):P * (k % 4 + 1)])
                last.then_inc(s("mixed"), 1)

            def main(c, o, start, stop, tiles=(0, KT)):
                dst = ps_l2(c, o)
                if start:
                    place_free(c, o)
                for k in range(*tiles):
                    if c == 0 and o % 2 == 0 and k % HALF == 0:
                        pe.wait_ge(s("w_lo"), 2 * (o // 2) + k // HALF + 1)
                    if o == 0:
                        pe.wait_ge(s("x_lo"), KT * c + k + 1)
                    cs = slice(P * o, P * (o + 1))
                    pe.matmul(dst, unit(k, 0)[:, cs], aT[:, k, 0, :], start=start and k == 0, stop=False)
                    pe.matmul(dst, unit(k, 0)[:, cs], aT[:, k, 1, :], start=False, stop=False)
                    last = pe.matmul(dst, unit(k, 1)[:, cs], aT[:, k, 0, :], start=False, stop=stop and k == KT - 1)
                    if o == KT - 1:
                        last.then_inc(s("steps"), 1)
                return last

            def place_free(c, o):
                if l2_before(c, o):
                    pe.wait_ge(s("x3"), l2_before(c, o))
                if o == 2 and c:
                    pe.wait_ge(s("x2"), CP * c)

            def low_rank(c):
                if c:
                    pe.wait_ge(s("low_sum"), c)
                for j in range(CP):
                    pe.wait_ge(s("a_lo"), CB * c + 2 * (j + 1))
                    for k in range(KT):
                        last = pe.matmul(ps_low[:, j // 2, 2 * P * (j % 2):2 * P * (j % 2 + 1)],
                                         a_sel[:, j, k, :, :, :].rearrange("p h t r -> p (h t r)"),
                                         aT[:, k, :, P * j:P * (j + 1)], start=(k == 0), stop=(k == KT - 1))
                last.then_inc(s("low"), 1)

            def delta(c, o, start, stop):
                if start:
                    place_free(c, o)
                return pe.matmul(ps_l2(c, o), b_split[:, P * o:P * (o + 1)], low_split[:, :], start=start, stop=stop)

            for k in range(KT):
                mix0(k)
            for c in range(CH):
                main(c, 0, True, False)
                low_rank(c)
                main(c, 1, True, False)
                main(c, 2, True, False, (0, HALF))
                pe.wait_ge(s("low_lo"), 2 * (c + 1))
                pe.wait_ge(s("low_hi"), 5 * (c + 1))
                pe.wait_ge(s("b_split"), 2)
                for o in range(2):
                    delta(c, o, False, True).then_inc(s("l2"), 1)
                delta(c, 2, False, False)
                for o in range(2, KT):
                    if o > 2:
                        last = delta(c, o, True, False)
                    if c == CH - 1 and o == KT - 1:
                        last.then_inc(s("delta"), 1)
                    last = main(c, o, False, True, (HALF if o == 2 else 0, KT))
                    if o < KT - 1:
                        last.then_inc(s("l2"), 1)
                    if c + 1 < CH and o - 2 < CP:
                        mix(CP * (c + 1) + o - 2)

            def slot(i):
                count8 = record(pe, i, THIS, 1, NA) * KT
                offs = [record(pe, i, f, 0, (RING - HALF) * UNIT) for f in (OFF_A, OFF_B)]
                pe.wait_ge(s("s_lo"), i + 2 if i else 1)
                if i >= 4:
                    pe.wait_ge(s("staged"), i - 3)
                for k in range(KT):
                    if i == 0 and k == HALF:
                        pe.wait_ge(s("s_lo"), 2)
                    pe.wait_ge(s("w_lo"), count8 + (k + 1))
                    off = offs[k // HALF] + (k % HALF) * UNIT
                    for m, part in ((0, 0), (0, 1), (1, 0)):
                        for n in range(2):
                            last = pe.matmul(ps[i % 4][:, n, :], aT[:, k, m, P * (i % 2):P * (i % 2 + 1)],
                                             ring[:, bass.ds(off + (part * D + n * 512), 512)],
                                             start=(k == 0 and m == 0 and part == 0),
                                             stop=(k == KT - 1 and m == 1))
                    last.then_inc(s("steps"), 1)

            pe.wait_ge(s("plan"), 1)
            slot_steps(pe, slot)


_OUT = (B + SLOTS, T, D)


def kernel(x, itok_B_0_15, itok_B_0_2, itok_B_3_7, L0_cond_weights, L1_cond_weights, L2_cond_W,
           L2_cond_lora_A, L2_cond_lora_B_w, L3_cond_weight):
    import concourse.bacc as bacc
    from concourse.bass_utils import run_bass_kernel_spmd

    lay = np.ascontiguousarray
    small, before, eyes = constants()
    w0 = np.asarray(L0_cond_weights).transpose(2, 0, 1)
    w1 = np.asarray(L1_cond_weights).transpose(1, 0, 2)
    la = np.asarray(L2_cond_lora_A).reshape(NL, KT, P, R).transpose(0, 2, 1, 3)
    lb = np.asarray(L2_cond_lora_B_w).transpose(1, 0)
    arrays = {
        "x": lay(x),
        "indices": lay(np.stack([np.asarray(i) for i in (itok_B_0_15, itok_B_0_2, itok_B_3_7)]).reshape(1, 3, B)),
        "w0t": lay(np.concatenate([w0[:, :, None, :]] * 2, axis=2).reshape(T, 2, D)),
        "w1": lay(w1.reshape(T, NC_ * T)),
        "wt": lay(np.asarray(L2_cond_W).transpose(1, 0)),
        "lora_a": lay(la.reshape(NL, P, KT * R)),
        "lora_b": lay(np.concatenate([lb] * (P // R), axis=0)),
        "w3t": lay(np.asarray(L3_cond_weight).transpose(0, 2, 1)),
        "small_c": small, "before_c": before, "eyes_c": eyes,
    }
    nc = bacc.Bacc("TRN2", target_bir_lowering=False, num_devices=1, dynamic_dma_scratch_size=1024)
    args = {n: nc.dram_tensor(n, a.shape, mybir.dt.from_np(a.dtype), kind="ExternalInput").ap() for n, a in arrays.items()}
    args["out"] = nc.dram_tensor("out", _OUT, F32, kind="ExternalOutput").ap()
    build(nc, **args)
    result = run_bass_kernel_spmd(nc, [arrays], core_ids=[0]).results[0]["out"]
    return result[0:B]
```

```python
import contextlib
import numpy as np
import concourse.bass as bass
from concourse import mybir

F32 = mybir.dt.float32
F32R = mybir.dt.float32r
I32 = mybir.dt.int32
ALU = mybir.AluOpType
ACT = mybir.ActivationFunctionType
AX = mybir.AxisListType

P = 128
B, T, D = 32, 64, 1024
NC_, NL, R, NA = 16, 5, 32, 8
KT = D // P
PAIRS = B // 2
CH = 4
CT = B * T // CH
CB = B // CH
CP = PAIRS // CH
SLOTS = B // 2 + NA // 2
SURE = B // 2
RAW = 4
RING = 12
UNIT = 2 * D
HALF = KT // 2
FIRST = "first"
WARM = 14
KEEP_WARM = 2
W_AFTER = {0: 0, 3: 1}
PLAN_STEPS = 8
EYES_AHEAD = 3

BATCH0, BATCH1, SINGLE = (0, 5), (5, 5), (10, 1)
LOAD_A, LOAD_B = (11, 1), (12, 1)
THIS = (13, 4)
PLACE_A, PLACE_B, NEXT_A = (17, 2), (19, 2), (21, 2)
NEXT_B = PLACE_A
WORD = 23
N_SLOTS, N_ACTIVE, ADAPTER = 0, 1, 2
HEAD = 16
C_E, C_S, C_B, C_LT8 = 0, NA, NA + SLOTS, NA + SLOTS + B
C_SIZE = C_LT8 + NA * NA


def constants():
    small = np.zeros((1, C_SIZE), np.float32)
    small[0, C_E:C_E + NA] = np.arange(NA)
    small[0, C_S:C_S + SLOTS] = np.arange(SLOTS)
    small[0, C_B:C_B + B] = np.arange(B)
    small[0, C_LT8:] = np.tril(np.ones((NA, NA), np.float32), -1).ravel()
    before = np.tril(np.ones((B, B), np.float32), -1).reshape(1, B * B)
    eye = np.eye(P, dtype=np.float32)
    return small, before, eye


def build(nc, x, indices, w0t, w1, wt, lora_a, lora_b, w3t, small_c, before_c, eye_c, out):
    at = [1152]

    def sb(name, shape, dtype, offset=None):
        size = 4 * int(np.prod(shape[1:]))
        if offset is None:
            offset = at[0]
            at[0] += (size + 31) // 32 * 32
        return nc.alloc_sbuf_tensor_at(name, shape, dtype, offset=offset)

    xT_at = at[0]
    xT = sb("xT", [P, KT, B * T], F32)
    aT_at = at[0]
    aT = sb("aT", [P, KT, 2, CT], F32R)
    ring_at = at[0]
    ring = sb("ring", [P, RING * UNIT], F32R)
    raw = sb("raw", [P, RAW, D], F32)
    eye = sb("eye", [P, P], F32)
    plan = sb("plan", [1, HEAD + SLOTS], I32)
    toks = sb("toks", [1, 3, B], I32)
    stage_at = at[0]
    stage = sb("stage", [P, 2, D], F32)
    mix_tab = sb("mix_tab", [P, NC_ * T], F32, offset=stage_at)
    mix_bd = sb("mix_bd", [P, 2 * CP, P], F32, offset=stage_at + 4 * NC_ * T)
    s_at = ring_at + 4 * UNIT * KT
    a_sel = sb("a_sel", [P, CP, KT, 2, 2, R], F32R, offset=s_at)
    s_at += 4 * CP * KT * 4 * R
    b_split = sb("b_split", [P, D], F32R, offset=s_at)
    s_at += 4 * D
    low_split = sb("low_split", [P, CT], F32R, offset=s_at)
    low = sb("low", [P, CT], F32, offset=s_at + 4 * CT)
    a_raw = sb("a_raw", [P, 2, KT * R], F32, offset=s_at + 8 * CT)
    assert s_at + 8 * CT + 8 * KT * R <= ring_at + 4 * UNIT * RING
    late = lambda k: xT[:, k, 2 * CT:4 * CT]
    small = xT[0:1, 0, 2 * CT:4 * CT]
    before = xT[0:1, 1, 2 * CT:4 * CT]
    w1_s = xT[0:T, 2, 2 * CT:4 * CT]
    w0_s = [xT[0:T, 3 + h, 2 * CT:4 * CT] for h in range(2)]
    b_raw = late(5)
    tmp = [xT[0:1, 6 + i, 2 * CT:4 * CT] for i in range(2)]
    half_w = lambda ap: ap.rearrange("p (k o) -> p k o", k=HALF)
    w_early = [half_w(late(6)), half_w(late(7)), xT[:, 0:HALF, CT + 256:2 * CT], xT[:, HALF:KT, CT + 256:2 * CT],
               half_w(late(3)), half_w(late(4))]
    EARLY = len(w_early)

    def unit(g, part):
        return ring[:, g * UNIT + part * D:g * UNIT + (part + 1) * D]

    ps = [nc.alloc_psum_tensor(f"ps{i}", [P, 2, 512], F32) for i in range(4)]
    ps_mix, ps_low = ps[0:2], ps[2]

    def l2_place(c, o):
        return (7 * c + o - (o > 2)) % 2 if o != 2 else 2

    def ps_l2(c, o):
        return ps_mix[1][:, 1, :] if o == 2 else ps[3][:, l2_place(c, o), :]

    def l2_before(c, o):
        n = [KT * d + q + 1 for d in range(CH) for q in range(KT)
             if (d, q) < (c, o) and l2_place(d, q) == l2_place(c, o)]
        return n[-1] if n else 0

    def x2_of(c, k):
        return ps_mix[k // 2 % 2][:, k % 2, :] if c == 0 else xT[:, k, CT * c:CT * (c + 1)]

    sem = {}

    def s(name):
        if name not in sem:
            sem[name] = nc.alloc_semaphore(name)
        return sem[name]

    raw_seq = [("x", p) for p in range(CP)] + [("w", u) for u in range(EARLY, KT)] + [("x", p) for p in range(CP, PAIRS)]
    raw_of = {e: n for n, e in enumerate(raw_seq)}
    RING_USES = len(raw_seq)

    def x3_split(slot, k, start, n):
        at_slot = 2 * P * (slot % 2) + start
        return aT[:, k, 0, at_slot:at_slot + n]

    aT_raw = sb("aT_raw", [P, KT, 2, CT], F32, offset=aT_at)

    def adapter_raw(t, first):
        if first or t < HALF:
            return raw[:, (RING_USES + t) % RAW, :].rearrange("p (q n) -> p q n", q=2)
        return aT_raw[:, 2 * (t - HALF):2 * (t - HALF) + 2, 1, :]

    def adapter_loaded(t, first, n):
        if first or t < HALF:
            slot = (RING_USES + t) % RAW
            loads_before = (RING_USES + t) // RAW
            if first:
                return s(f"raw{slot}"), 16 * (loads_before + 1)
            total_first = len([u for u in range(RING_USES + KT) if u % RAW == slot])
            return s(f"raw{slot}"), n * 16 + 16 * total_first
        return s(f"a_hold{t}"), n * 16

    def in_two(ap):
        return ap.rearrange("p (q n) -> p q n", q=2)

    def wait_raw(eng, entry):
        n = raw_of[entry]
        eng.wait_ge(s(f"raw{n % RAW}"), 16 * (n // RAW + 1))

    def raw_tile(entry):
        return raw[:, raw_of[entry] % RAW, :]

    def w_unit(u):
        return u // 2, u % 2

    def w_raw(u):
        return w_early[u] if u < EARLY else raw_tile(("w", u)).rearrange("p (k o) -> p k o", k=HALF)

    def wait_w(eng, u):
        if u < EARLY:
            eng.wait_ge(s(f"w_raw{u}"), 16)
        else:
            wait_raw(eng, ("w", u))

    def low_parts_of(part):
        return ps_low[:, :, :].rearrange("p a (j t n) -> p (a j) t n", t=2, n=P)[:, :, part, :]

    def of_batch(ap, h):
        return ap.rearrange("p (j h n) -> p j h n", h=2, n=T)[:, :, h, :]

    def a_raw_of(b):
        if b < CB:
            return xT[:, b, CT:CT + KT * R], s(f"a_raw{b}"), 16
        return a_raw[:, b % 2, :], s(f"a_ring{b % 2}"), 16 * ((b - CB) // 2 + 1)

    def w_diagonals(u):
        q, h = w_unit(u)
        return [k for k in (2 * q, 2 * q + 1) if k // HALF == h]

    def w_dst(u, part):
        q, h = w_unit(u)
        v = ring[:, :].rearrange("p (g t n) -> p g t n", t=2, n=D)
        return v[:, HALF * h:HALF * (h + 1), part, 256 * q:256 * (q + 1)]

    def slot_word(eng, slot):
        return eng.value_load(plan[0:1, HEAD + slot:HEAD + slot + 1], min_val=0, max_val=2 ** WORD - 1)

    def get(word, field):
        return (word >> field[0]) & (2 ** field[1] - 1)

    def batches(word):
        return [get(word, BATCH0), get(word, BATCH1)]

    def ring_place(eng, word, field):
        return nc.s_assert_within(eng.snap(get(word, field) * (HALF * UNIT)), 0, (RING - HALF) * UNIT)

    def head(eng, i, lo, hi):
        return eng.value_load(plan[0:1, i:i + 1], min_val=lo, max_val=hi)

    BEFORE3 = 8 * CH

    with nc.Block() as block:

        @block.sync
        def _(sp):
            xp = x.rearrange("(q two) t d -> q (two t) d", two=2)
            wv = wt.rearrange("(k p) o -> p k o", p=P)

            def raw_free(n):
                if n >= RAW:
                    kind, i = raw_seq[n - RAW] if n - RAW < len(raw_seq) else ("a", n - RAW - len(raw_seq))
                    if kind == "x" and i < CP:
                        sp.wait_ge(s("mixed0"), KT)
                    elif kind == "x":
                        sp.wait_ge(s("mixed"), i - CP + 1)
                    else:
                        sp.wait_ge(s("w_lo"), i + 1 if kind == "w" else KT + i + 1)

            def load_raw(entry):
                n = raw_of[entry]
                raw_free(n)
                kind, i = entry
                dst, src = (raw[:, n % RAW, :], xp[i, :, :]) if kind == "x" else (w_raw(i), w_src(i))
                sp.dma_start(dst, src).then_inc(s(f"raw{n % RAW}"), 16)

            def w_src(u):
                q, h = w_unit(u)
                return wv[:, HALF * h:HALF * (h + 1), 256 * q:256 * (q + 1)]

            def load_a(b):
                if b >= CB + 2:
                    sp.wait_ge(s("a_lo"), b - 1)
                dst, loaded, _ = a_raw_of(b)
                l = sp.value_load(toks[0:1, 1, b:b + 1], min_val=0, max_val=NL - 1)
                sp.dma_start(dst, lora_a[bass.ds(l, 1), :, :].rearrange("a p n -> p (a n)")).then_inc(loaded, 16)

            sp.dma_start(w1_s, w1).then_inc(s("w1"), 16)
            for h in range(2):
                sp.dma_start(w0_s[h], w0t[:, h, :]).then_inc(s(f"w0_{h}"), 16)
            for e in raw_seq[0:CP]:
                load_raw(e)

            def load_w(u):
                sp.dma_start(w_early[u], w_src(u)).then_inc(s(f"w_raw{u}"), 16)

            load_w(0)
            load_w(1)
            sp.wait_ge(s("toks"), 16)
            for b in range(CB):
                load_a(b)
            load_w(2)
            load_w(3)
            sp.dma_start(b_raw, lora_b).then_inc(s("b_raw"), 16)
            sp.wait_ge(s("mm"), 2)
            load_w(4)
            load_w(5)
            sp.dma_start(small[:, 0:C_SIZE], small_c).then_inc(s("consts"), 16)
            sp.dma_start(before, before_c).then_inc(s("consts"), 16)
            for e in raw_seq[CP:CP + KT - EARLY]:
                load_raw(e)
            for c in range(1, CH):
                for j in range(CP):
                    load_raw(("x", c * CP + j))
                    load_a(c * CB + 2 * j)
                    load_a(c * CB + 2 * j + 1)
            sp.wait_ge(s("plan"), 1)
            n_active = head(sp, N_ACTIVE, 1, NA)
            for k in range(NA):
                def load_adapter(k=k):
                    e = head(sp, ADAPTER + k, 0, NA - 1)
                    for t in range(KT):
                        if k == 0:
                            raw_free(RING_USES + t)
                        else:
                            if t < HALF:
                                last = KT * k + max(u for u in range(KT) if (u - t) % RAW == 0 and (k == 1 or u < HALF))
                            else:
                                last = KT * k + t
                            if k > 1 or t < HALF:
                                sp.wait_ge(s("w_lo"), last + 1)
                            elif t == HALF:
                                sp.wait_ge(s("steps"), BEFORE3)
                        src = w3t[bass.ds(e, 1), t * P:(t + 1) * P, :].rearrange("a p (q n) -> p (a q) n", q=2)
                        loaded, _ = adapter_loaded(t, k == 0, k)
                        sp.dma_start(adapter_raw(t, k == 0), src).then_inc(loaded, 16)
                if k == 0:
                    load_adapter()
                else:
                    with sp.If(n_active > k):
                        load_adapter()

        @block.gpsimd
        def _(pool):
            pool.memset(mix_bd[:, 0:1, :], 0.0).then_inc(s("zeroed"), 1)
            pool.memset(mix_bd[:, 1:2 * CP, :], 0.0).then_inc(s("zeroed"), 1)
            pool.wait_ge(s("toks"), 16)

            def condition(b):
                return pool.value_load(toks[0:1, 0, b:b + 1], min_val=0, max_val=NC_ - 1)

            ahead = [condition(b) for b in range(CB, 2 * CB)]
            pool.wait_ge(s("zeroed"), 2)
            pool.wait_ge(s("mix_tab"), 2)
            for p in range(CP, PAIRS):
                if 2 * CP <= p < 3 * CP:
                    pool.wait_ge(s("mixed0"), KT)
                elif p >= 3 * CP:
                    pool.wait_ge(s("mixed"), p - 3 * CP + 1)
                for h in range(2):
                    b = 2 * p + h
                    c = ahead[b - CB] if b < 2 * CB else condition(b)
                    rows = slice(h * T, (h + 1) * T)
                    pool.tensor_copy(mix_bd[rows, p % (2 * CP), h * T:(h + 1) * T],
                                     mix_tab[rows, bass.ds(c * T, T)]).then_inc(s("bd"), 1)

        @block.scalar
        def _(act):
            act.dma_start(eye[:, :], eye_c).then_inc(s("eye"), 16)
            act.dma_start(toks[:, :, :], indices).then_inc(s("toks"), 16)

            def mix_out(p):
                act.wait_ge(s("mixed"), p - CP + 1)
                if p == CP:
                    act.wait_ge(s("w_lo"), EARLY)
                    act.wait_ge(s("a_lo"), CB)
                if p == 2 * CP:
                    act.wait_ge(s("plan"), 1)
                    act.wait_ge(s("b_split"), 2)
                act.activation(xT[:, :, P * p:P * (p + 1)],
                               ps_mix[p % 2][:, :, :].rearrange("p a (k n) -> p (a k) n", n=P), ACT.Copy)\
                   .then_inc(s("x2"), 1)

            def w_hi(u):
                if w_diagonals(u):
                    act.wait_ge(s("w_eye"), sum(len(w_diagonals(v)) for v in range(u + 1)))
                else:
                    wait_w(act, u)
                act.activation(w_dst(u, 0), w_raw(u), ACT.Copy)\
                   .then_inc(s("w_hi"), 1)

            def a_hi(c, k):
                if c:
                    act.wait_ge(s("x2"), CP * c)
                    act.wait_ge(s("steps"), KT * (c - 1) + k + 1)
                else:
                    act.wait_ge(s("mixed0"), k + 1)
                act.activation(aT[:, k, 0, :], x2_of(c, k), ACT.Copy).then_inc(s("x_hi"), 1)

            def lora_hi(b):
                src, loaded, value = a_raw_of(b)
                act.wait_ge(loaded, value)
                act.wait_ge(s("low"), b // CB)
                act.activation(a_sel[:, b % CB // 2, :, b % 2, 0, :],
                               src.rearrange("p (k r) -> p k r", r=R), ACT.Copy).then_inc(s("a_hi"), 1)

            def low_out(c):
                act.wait_ge(s("low"), c + 1)
                act.activation(low[:, :].rearrange("p (j n) -> p j n", n=P), low_parts_of(1), ACT.Copy).then_inc(s("low_cols"), 1)
                act.wait_ge(s("low_sum"), c + 1)
                act.wait_ge(s("steps"), KT * c)
                for h, src, dst, n in ((0, 0, 0, 2), (1, 2, 2, 1), (1, 2, 0, 2), (0, 0, 3, 1), (1, 2, 3, 1)):
                    act.activation(of_batch(low_split[R * dst:R * (dst + n), :], h),
                                   of_batch(low[R * src:R * (src + n), :], h), ACT.Copy).then_inc(s("low_hi"), 1)

            def l2_out(c, o):
                if o < KT - 1:
                    act.wait_ge(s("l2"), (KT - 1) * c + o + 1)
                else:
                    act.wait_ge(s("steps"), KT * (c + 1))
                act.activation(xT[:, o, CT * c:CT * (c + 1)], ps_l2(c, o), ACT.Copy).then_inc(s("x3"), 1)

            for k in range(KT):
                a_hi(0, k)
                if k in W_AFTER:
                    w_hi(W_AFTER[k])
                if k == HALF:
                    act.wait_ge(s("bd"), CB)
                    for h in range(2):
                        act.activation(mix_tab[:, 512 * h:512 * (h + 1)], ps_low[:, h, :], ACT.Copy).then_inc(s("mix_tab"), 1)
            for b in range(CB):
                lora_hi(b)
            w_hi(2)
            w_hi(3)
            act.wait_ge(s("b_raw"), 16)
            act.activation(b_split[:, :], b_raw, ACT.Copy, scale=0.5).then_inc(s("b_split"), 1)
            w_hi(4)
            w_hi(5)

            def adapter_hi(k, t, dst, count8):
                act.wait_ge(s("w_eye"), count8 + (t + 1))
                act.activation(dst, adapter_raw(t, k == 0), ACT.Copy).then_inc(s("w_hi"), 1)

            for c in range(CH):
                low_out(c)
                if c == 0:
                    w_hi(6)
                    w_hi(7)
                l2_out(c, 0)
                l2_out(c, 1)
                for o in range(2, KT - 1):
                    l2_out(c, o)
                    if c + 1 < CH:
                        if o - 2 < CP:
                            mix_out(CP * (c + 1) + o - 2)
                        for b in range(2 * (o - 2), min(2 * (o - 1), CB)):
                            lora_hi(CB * (c + 1) + b)
                    elif o < 4:
                        act.wait_ge(s("low"), CH)
                        adapter_hi(0, o - 2, in_two(unit(KT + o - 2, 0)), KT)
                if c + 1 < CH:
                    for k in range(KT):
                        a_hi(c + 1, k)
                else:
                    act.wait_ge(s("delta"), 1)
                    for t in range(2, HALF):
                        adapter_hi(0, t, in_two(unit(KT + t, 0)), KT)
                if c + 1 < CH:
                    l2_out(c, KT - 1)

            def slot_hi(i, word, tiles=(0, KT)):
                which = batches(word)
                ks = slice(*tiles)
                act.wait_ge(s("steps"), BEFORE3 + (KT * (i - 1) if i else tiles[1] - KT))
                for h in range(2):
                    act.activation(x3_split(i, ks, h * T, T), xT[:, ks, bass.ds(which[h] * T, T)], ACT.Copy).then_inc(s("s_hi"), 1)

            def slot_out(i, word):
                single = get(word, SINGLE)
                act.wait_ge(s("steps"), BEFORE3 + KT * (i + 1))
                if i >= 2:
                    act.wait_ge(s(f"stored{i - 2}"), 32)
                result = ps[i % 4][:, :, :].rearrange("p a n -> p (a n)")
                with act.If(single < 1):
                    act.activation(stage[:, i % 2, :], result, ACT.Copy).then_inc(s("staged"), 1)
                with act.If(single > 0):
                    act.activation(stage[0:T, i % 2, :], result[T:P, :], ACT.Copy).then_inc(s(f"lo_rows{i}"), 1)

            def store(i, word):
                rows, single = batches(word), get(word, SINGLE)
                act.wait_ge(s("staged"), i + 1)
                with act.If(single < 1):
                    for h in range(2):
                        act.dma_start(out[bass.ds(rows[h], 1), :, :].rearrange("a t d -> (a t) d"),
                                      stage[h * T:(h + 1) * T, i % 2, :]).then_inc(s(f"stored{i}"), 16)
                with act.If(single > 0):
                    for t in range(0, T, T // 2):
                        act.dma_start(out[bass.ds(rows[0], 1), t:t + T // 2, :].rearrange("a t d -> (a t) d"),
                                      stage[t:t + T // 2, i % 2, :]).then_inc(s(f"stored{i}"), 16)

            act.wait_ge(s("plan"), 1)
            act.wait_ge(s("x3"), KT * CH - 1)
            word = slot_word(act, 0)
            slot_hi(0, word, (0, HALF))
            l2_out(CH - 1, KT - 1)
            act.wait_ge(s("x3"), KT * CH)
            slot_hi(0, word, (HALF, KT))
            for t in range(HALF, KT):
                adapter_hi(0, t, in_two(unit(t - HALF, 0)), KT)
            n_slots = head(act, N_SLOTS, SURE, SLOTS)

            def step(i, earlier, word):
                following = slot_word(act, i + 1) if i + 1 < SLOTS else None
                if i + 1 < SURE:
                    slot_hi(i + 1, following)
                elif i + 1 < SLOTS:
                    with act.If(n_slots > i + 1):
                        slot_hi(i + 1, following)
                if i:
                    slot_out(i - 1, earlier)
                for flag, place, t0 in ((LOAD_A, NEXT_A, 0), (LOAD_B, NEXT_B, HALF)):
                    with act.If(get(word, flag) > 0):
                        count8 = act.snap((get(word, THIS) + 1) * KT)
                        off = ring_place(act, word, place)
                        for t in range(t0, t0 + HALF):
                            done = KT * (i - 1) + t + HALF + 1 if t0 == 0 else KT * i + t - HALF + 1
                            act.wait_ge(s("steps"), BEFORE3 + done)
                            adapter_hi(None, t, in_two(ring[:, bass.ds(off + (t - t0) * UNIT, D)]), count8)
                if i:
                    store(i - 1, earlier)
                return word, following

            earlier = None
            for i in range(SURE):
                earlier, word = step(i, earlier, word)
            with contextlib.ExitStack() as nested:
                for i in range(SURE, SLOTS):
                    with act.If(n_slots == i):
                        slot_out(i - 1, earlier)
                        store(i - 1, earlier)
                    nested.enter_context(act.If(n_slots > i))
                    earlier, word = step(i, earlier, word)
                slot_out(SLOTS - 1, earlier)
                store(SLOTS - 1, earlier)
            for i in range(SLOTS):
                if i < SURE:
                    act.wait_ge(s(f"stored{i}"), 32)
                else:
                    with act.If(n_slots > i):
                        act.wait_ge(s(f"stored{i}"), 32)

        @block.vector
        def _(dve):
            as_f32 = lambda ap: ap.bitcast(F32)
            dve.wait_ge(s("eye"), 16)
            for h in range(2):
                v1 = w1_s[:, 512 * h:512 * (h + 1)].rearrange("p (c n) -> p c n", n=T)
                v0 = w0_s[h].rearrange("p (c n) -> p c n", n=T)
                for v, loaded in ((v1, "w1"), (v0, f"w0_{h}")):
                    dve.wait_ge(s(loaded), 16)
                    dve.tensor_tensor(v, v, eye[0:T, 0:T].unsqueeze(1).to_broadcast([T, v.shape[1], T]), ALU.add)\
                       .then_inc(s("w01i"), 1)

            dve.wait_ge(s("toks"), 16)
            ahead = [dve.value_load(toks[0:1, 0, b:b + 1], min_val=0, max_val=NC_ - 1) for b in range(CB)]
            dve.wait_ge(s("zeroed"), 2)
            dve.wait_ge(s("mm"), 2)
            table = ps_low[:, :, :].rearrange("p a n -> p (a n)")
            for b in range(CB):
                rows = slice(b % 2 * T, (b % 2 + 1) * T)
                dve.tensor_copy(mix_bd[rows, b // 2, b % 2 * T:(b % 2 + 1) * T], table[rows, bass.ds(ahead[b] * T, T)])\
                   .then_inc(s("bd"), 1)

            def add_eye(dst):
                dve.tensor_tensor(dst, dst, eye[:, :], ALU.add).then_inc(s("w_eye"), 1)

            def w_eye(u):
                if w_diagonals(u):
                    wait_w(dve, u)
                q, h = w_unit(u)
                for k in w_diagonals(u):
                    add_eye(w_raw(u)[:, k - HALF * h, (k - 2 * q) * P:(k - 2 * q + 1) * P])

            def w_lo(u):
                dve.wait_ge(s("w_hi"), u + 1)
                dve.tensor_tensor(w_dst(u, 1), w_raw(u), as_f32(w_dst(u, 0)), ALU.subtract).then_inc(s("w_lo"), 1)

            def w_pair(u):
                w_eye(u)
                w_eye(u + 1)
                w_lo(u)
                w_lo(u + 1)

            def a_lo(c, k):
                dve.wait_ge(s("x_hi"), KT * c + k + 1)
                dve.tensor_tensor(aT[:, k, 1, :], x2_of(c, k), as_f32(aT[:, k, 0, :]), ALU.subtract)\
                   .then_inc(s("x_lo"), 1)

            def lora_lo(b):
                dve.wait_ge(s("a_hi"), b + 1)
                v = a_sel[:, b % CB // 2, :, b % 2, :, :]
                dve.tensor_tensor(v[:, :, 1, :], a_raw_of(b)[0].rearrange("p (k r) -> p k r", r=R),
                                  as_f32(v[:, :, 0, :]), ALU.subtract).then_inc(s("a_lo"), 1)

            def low_parts(c):
                v = low[:, :].rearrange("p (j n) -> p j n", n=P)
                dve.wait_ge(s("low_cols"), c + 1)
                dve.tensor_tensor(v, low_parts_of(0), v, ALU.add).then_inc(s("low_sum"), 1)
                for h, src in ((0, 0), (1, 2)):
                    dve.wait_ge(s("low_hi"), 5 * c + h + 1)
                    rows = slice(R * src, R * (src + 1))
                    dve.tensor_tensor(of_batch(low_split[2 * R:3 * R, :], h), of_batch(low[rows, :], h),
                                      as_f32(of_batch(low_split[rows, :], h)), ALU.subtract).then_inc(s("low_lo"), 1)

            def make_plan():
                steps = []
                def do(emit, *args):
                    steps.append((emit, args))

                used = [C_SIZE]

                def cells(n):
                    used[0] += n
                    assert used[0] <= D
                    return small[:, used[0] - n:used[0]]

                def rows(ap, n, m):
                    return ap.unsqueeze(1).to_broadcast([1, n, m])

                def cols(ap, n, m):
                    return ap.unsqueeze(2).to_broadcast([1, n, m])

                def grid(i, n, m):
                    return tmp[i][:, 0:n * m].rearrange("o (n m) -> o n m", m=m)

                def tt(dst, a, b, op):
                    do(dve.tensor_tensor, dst, a, b, op)

                def ts(dst, a, k1, op1, k2=None, op2=None):
                    do(dve.tensor_scalar, dst, a, k1, k2, *((op1,) if op2 is None else (op1, op2)))

                def total(dst, src):
                    do(dve.reduce_sum, dst, src, AX.X)

                def weighted(dst, g, weights, n, m, spare=1):
                    tt(grid(spare, n, m), g, weights, ALU.mult)
                    total(dst, grid(spare, n, m))

                e, slot, bat = small[:, C_E:C_E + NA], small[:, C_S:C_S + SLOTS], small[:, C_B:C_B + B]
                below = small[:, C_LT8:C_LT8 + NA * NA].rearrange("o (n m) -> o n m", m=NA)
                a = cells(B)
                do(dve.tensor_copy, a, toks[0:1, 2, :])
                cnt, half, occurs = cells(NA), cells(NA), cells(NA)
                tt(grid(0, NA, B), cols(e, NA, B), rows(a, NA, B), ALU.is_equal)
                total(cnt, grid(0, NA, B))
                whole = cells(NA).bitcast(I32)
                ts(whole, cnt, 1.0, ALU.add)
                ts(whole, whole, 1, ALU.logical_shift_right)
                do(dve.tensor_copy, half, whole)
                ts(occurs, cnt, 1.0, ALU.min)
                first, order, last = cells(NA), cells(NA), cells(NA)
                weighted(first, below, rows(half, NA, NA), NA, NA)
                weighted(order, below, rows(occurs, NA, NA), NA, NA)
                tt(last, first, half, ALU.add)
                ts(last, last, -1.0, ALU.add)
                place, rank = cells(B), cells(B)
                tt(grid(0, B, B), cols(a, B, B), rows(a, B, B), ALU.is_equal)
                weighted(rank, grid(0, B, B), before.rearrange("o (n m) -> o n m", m=B), B, B)
                tt(grid(0, B, NA), cols(a, B, NA), rows(e, B, NA), ALU.is_equal)
                weighted(place, grid(0, B, NA), rows(first, B, NA), B, NA)
                ts(place, place, 2.0, ALU.mult)
                tt(place, place, rank, ALU.add)
                S = SLOTS
                twice, b0, b1, there, mine = cells(S), cells(S), cells(S), cells(S), cells(S)
                ts(twice, slot, 2.0, ALU.mult)
                tt(grid(0, S, B), cols(twice, S, B), rows(place, S, B), ALU.is_equal)
                weighted(b0, grid(0, S, B), rows(bat, S, B), S, B)
                weighted(mine, grid(0, S, B), rows(a, S, B), S, B)
                ts(twice, twice, 1.0, ALU.add)
                tt(grid(0, S, B), cols(twice, S, B), rows(place, S, B), ALU.is_equal)
                total(there, grid(0, S, B))
                weighted(b1, grid(0, S, B), rows(bat, S, B), S, B)
                single, again = cells(S), cells(S)
                ts(single, there, -1.0, ALU.mult, 1.0, ALU.add)
                tt(again, single, b0, ALU.mult)
                tt(b1, b1, again, ALU.add)
                nth, lo, hi = cells(S), cells(S), cells(S)
                tt(grid(0, S, NA), cols(mine, S, NA), rows(e, S, NA), ALU.is_equal)
                weighted(nth, grid(0, S, NA), rows(order, S, NA), S, NA)
                weighted(lo, grid(0, S, NA), rows(first, S, NA), S, NA)
                weighted(hi, grid(0, S, NA), rows(last, S, NA), S, NA)
                n_slots, n_active = cells(1), cells(1)
                total(n_slots, half)
                total(n_active, occurs)
                more = cells(S)
                ts(more, nth, 1.0, ALU.add)
                tt(more, more, n_active.to_broadcast([1, S]), ALU.is_lt)
                tt(lo, lo, slot, ALU.is_equal)
                tt(lo, lo, more, ALU.mult)
                tt(hi, hi, slot, ALU.is_equal)
                tt(hi, hi, more, ALU.mult)
                word, fixed = cells(S), 0

                def put(field, src, factor=1.0):
                    do(dve.scalar_tensor_tensor, word, src, factor * 2.0 ** field[0], word, ALU.mult, ALU.add)

                ts(word, b0, 2.0 ** BATCH0[0], ALU.mult)
                put(BATCH1, b1)
                put(SINGLE, single)
                put(LOAD_A, lo)
                put(LOAD_B, hi)
                put(THIS, nth)
                fixed += 1 << THIS[0]
                mod3, wraps = cells(S), cells(S)
                for field, ahead in ((PLACE_A, 0), (NEXT_A, 1), (PLACE_B, 2)):
                    ts(mod3, nth, float(ahead), ALU.add)
                    for m in (3, 6, 9):
                        ts(wraps, nth, float(m - ahead), ALU.is_ge, -3.0, ALU.mult)
                        tt(mod3, mod3, wraps, ALU.add)
                    put(field, mod3, -1.0)
                    fixed += 2 << field[0]
                ts(plan[:, HEAD:HEAD + S], word, float(fixed), ALU.add)
                tt(grid(0, NA, NA), cols(e, NA, NA), rows(order, NA, NA), ALU.is_equal)
                tt(grid(0, NA, NA), grid(0, NA, NA), rows(occurs, NA, NA), ALU.mult)
                ids = cells(NA)
                weighted(ids, grid(0, NA, NA), rows(e, NA, NA), NA, NA)
                do(dve.tensor_copy, plan[:, ADAPTER:ADAPTER + NA], ids)
                do(dve.tensor_copy, plan[:, N_SLOTS:N_SLOTS + 1], n_slots)
                do(dve.tensor_copy, plan[:, N_ACTIVE:N_ACTIVE + 1], n_active)
                return steps

            def take(steps, done, n):
                for emit, args in steps[done:done + n]:
                    dve.wait_ge(s("chain"), done)
                    done += 1
                    emit(*args).then_inc(s("plan" if done == len(steps) else "chain"), 1)
                return done

            w_eye(0)
            for k in range(KT):
                a_lo(0, k)
                if k in W_AFTER:
                    w_lo(W_AFTER[k])
                if k == 1:
                    w_eye(1)
            for b in range(CB):
                lora_lo(b)
            w_pair(2)
            dve.wait_ge(s("b_split"), 1)
            dve.scalar_tensor_tensor(b_split[3 * R:, :], b_raw[3 * R:, :], 0.5, as_f32(b_split[3 * R:, :]),
                                     ALU.mult, ALU.subtract).then_inc(s("b_split"), 1)
            w_pair(4)

            def adapter_half(t0, n, unit_of):
                first = n is FIRST
                n = 0 if first else n
                for t in range(t0, t0 + HALF + EYES_AHEAD):
                    if t < t0 + HALF:
                        dve.wait_ge(*adapter_loaded(t, first, n))
                        q, col = divmod(P * t, D // 2)
                        add_eye(adapter_raw(t, first)[:, q, col:col + P])
                    u = t - EYES_AHEAD
                    if u >= t0:
                        dve.wait_ge(s("w_hi"), n * KT + (KT + u + 1))
                        dve.tensor_tensor(in_two(unit_of(u, 1)), adapter_raw(u, first),
                                          as_f32(in_two(unit_of(u, 0))), ALU.subtract).then_inc(s("w_lo"), 1)

            for c in range(CH):
                low_parts(c)
                if c == 1:
                    done = take(steps, done, len(steps))
                if c == 0:
                    w_pair(6)
                    steps, done = make_plan(), 0
                    dve.wait_ge(s("consts"), 32)
                    dve.wait_ge(s("toks"), 16)
                if c + 1 < CH:
                    for b in range(CB * (c + 1), CB * (c + 2)):
                        lora_lo(b)
                        if c == 0:
                            done = take(steps, done, PLAN_STEPS)
                    for k in range(KT):
                        a_lo(c + 1, k)

            adapter_half(0, FIRST, lambda t, part: unit(KT + t, part))

            def slot_lo(i, word, tiles=(0, KT)):
                which = batches(word)
                ks = slice(*tiles)
                earlier = 2 * i + 2 if i else 2 * (tiles[0] // HALF)
                for h in range(2):
                    dve.wait_ge(s("s_hi"), earlier + h + 1)
                    ins = dve.tensor_tensor(x3_split(i, ks, P + h * T, T), xT[:, ks, bass.ds(which[h] * T, T)],
                                            as_f32(x3_split(i, ks, h * T, T)), ALU.subtract)
                ins.then_inc(s("s_lo"), 1)

            word = slot_word(dve, 0)
            slot_lo(0, word, (0, HALF))
            slot_lo(0, word, (HALF, KT))
            adapter_half(HALF, FIRST, lambda t, part: unit(t - HALF, part))
            n_slots = head(dve, N_SLOTS, SURE, SLOTS)

            def single_sum(i, word):
                with dve.If(get(word, SINGLE) > 0):
                    dve.wait_ge(s(f"lo_rows{i}"), 1)
                    dst = stage[0:T, i % 2, :]
                    dve.tensor_tensor(dst, ps[i % 4][0:T, :, :].rearrange("p a n -> p (a n)"), dst, ALU.add)\
                       .then_inc(s("staged"), 1)

            def step(i, earlier, word):
                following = slot_word(dve, i + 1) if i + 1 < SLOTS else None
                if i + 1 < SURE:
                    slot_lo(i + 1, following)
                elif i + 1 < SLOTS:
                    with dve.If(n_slots > i + 1):
                        slot_lo(i + 1, following)
                if i:
                    single_sum(i - 1, earlier)
                for flag, place, t0 in ((LOAD_A, NEXT_A, 0), (LOAD_B, NEXT_B, HALF)):
                    with dve.If(get(word, flag) > 0):
                        n = dve.snap(get(word, THIS))
                        off = ring_place(dve, word, place)
                        adapter_half(t0, n, lambda t, part: ring[:, bass.ds(off + (t - t0) * UNIT + part * D, D)])
                return word, following

            earlier = None
            for i in range(SURE):
                earlier, word = step(i, earlier, word)
            with contextlib.ExitStack() as nested:
                for i in range(SURE, SLOTS):
                    with dve.If(n_slots == i):
                        single_sum(i - 1, earlier)
                    nested.enter_context(dve.If(n_slots > i))
                    earlier, word = step(i, earlier, word)
                single_sum(SLOTS - 1, earlier)

        @block.tensor
        def _(pe):
            pe.wait_ge(s("zeroed"), 1)
            for i in range(WARM):
                pe.matmul(ps[3][:, 0, 0:P], mix_bd[:, 0, :], mix_bd[:, 0, :], start=True, stop=True)

            for h in range(2):
                pe.wait_ge(s("w01i"), 2 * (h + 1))
                cols8 = w1_s[:, 512 * h:512 * (h + 1)]
                for c in range(8):
                    last = pe.matmul(ps_low[:, h, T * c:T * (c + 1)], w0_s[h][:, P * c:P * (c + 1)],
                                     cols8[:, T * c:T * (c + 1)], start=True, stop=True)
                last.then_inc(s("mm"), 1)

            pe.wait_ge(s("eye"), 16)
            for i in range(KEEP_WARM):
                pe.matmul(ps[3][:, 0, 0:P], eye[:, :], eye[:, :], start=True, stop=True)

            def mix_tile(p, k, dst):
                return pe.matmul(dst, raw_tile(("x", p))[:, P * k:P * (k + 1)], mix_bd[:, p % (2 * CP), :],
                                 start=True, stop=True)

            def mix0(k):
                if k >= 4:
                    pe.wait_ge(s("x_lo"), k - 3)
                for p in range(CP):
                    if k == 0:
                        wait_raw(pe, ("x", p))
                        pe.wait_ge(s("bd"), 2 * (p + 1))
                    last = mix_tile(p, k, x2_of(0, k)[:, P * p:P * (p + 1)])
                last.then_inc(s("mixed0"), 1)

            def mix(p):
                wait_raw(pe, ("x", p))
                pe.wait_ge(s("bd"), 2 * (p + 1))
                if p >= CP + 2:
                    pe.wait_ge(s("x2"), p - CP - 1)
                if p % 2:
                    pe.wait_ge(s("x3"), KT * (p // CP - 1) + 3)
                for k in range(KT):
                    last = mix_tile(p, k, ps_mix[p % 2][:, k // 4, P * (k % 4):P * (k % 4 + 1)])
                last.then_inc(s("mixed"), 1)

            def main(c, o, start, stop, tiles=(0, KT)):
                dst = ps_l2(c, o)
                if start:
                    place_free(c, o)
                for k in range(*tiles):
                    if c == 0 and o % 2 == 0 and k % HALF == 0:
                        pe.wait_ge(s("w_lo"), 2 * (o // 2) + k // HALF + 1)
                    if o == 0:
                        pe.wait_ge(s("x_lo"), KT * c + k + 1)
                    cs = slice(P * o, P * (o + 1))
                    pe.matmul(dst, unit(k, 0)[:, cs], aT[:, k, 0, :], start=start and k == 0, stop=False)
                    pe.matmul(dst, unit(k, 0)[:, cs], aT[:, k, 1, :], start=False, stop=False)
                    last = pe.matmul(dst, unit(k, 1)[:, cs], aT[:, k, 0, :], start=False, stop=stop and k == KT - 1)
                    if o == KT - 1:
                        last.then_inc(s("steps"), 1)
                return last

            def place_free(c, o):
                if l2_before(c, o):
                    pe.wait_ge(s("x3"), l2_before(c, o))
                if o == 2 and c:
                    pe.wait_ge(s("x2"), CP * c)

            def low_rank(c):
                if c:
                    pe.wait_ge(s("low_sum"), c)
                for j in range(CP):
                    pe.wait_ge(s("a_lo"), CB * c + 2 * (j + 1))
                    for k in range(KT):
                        last = pe.matmul(ps_low[:, j // 2, 2 * P * (j % 2):2 * P * (j % 2 + 1)],
                                         a_sel[:, j, k, :, :, :].rearrange("p h t r -> p (h t r)"),
                                         aT[:, k, :, P * j:P * (j + 1)], start=(k == 0), stop=(k == KT - 1))
                last.then_inc(s("low"), 1)

            def delta(c, o, start, stop):
                if start:
                    place_free(c, o)
                return pe.matmul(ps_l2(c, o), b_split[:, P * o:P * (o + 1)], low_split[:, :], start=start, stop=stop)

            for k in range(KT):
                mix0(k)
            for c in range(CH):
                main(c, 0, True, False)
                low_rank(c)
                main(c, 1, True, False)
                main(c, 2, True, False, (0, HALF))
                pe.wait_ge(s("low_lo"), 2 * (c + 1))
                pe.wait_ge(s("low_hi"), 5 * (c + 1))
                pe.wait_ge(s("b_split"), 2)
                for o in range(2):
                    delta(c, o, False, True).then_inc(s("l2"), 1)
                delta(c, 2, False, False)
                for o in range(2, KT):
                    if o > 2:
                        last = delta(c, o, True, False)
                    if c == CH - 1 and o == KT - 1:
                        last.then_inc(s("delta"), 1)
                    last = main(c, o, False, True, (HALF if o == 2 else 0, KT))
                    if o < KT - 1:
                        last.then_inc(s("l2"), 1)
                    if c + 1 < CH and o - 2 < CP:
                        mix(CP * (c + 1) + o - 2)

            def slot_record(i):
                word = slot_word(pe, i)
                return (pe.snap(get(word, THIS) * KT), [ring_place(pe, word, f) for f in (PLACE_A, PLACE_B)],
                        get(word, SINGLE))

            def products(i, mine, passes, half):
                count8, offs, _ = mine
                for k in range(HALF * half, HALF * (half + 1)):
                    if i == 0 and k == HALF:
                        pe.wait_ge(s("s_lo"), 2)
                    pe.wait_ge(s("w_lo"), count8 + (k + 1))
                    off = offs[half] + (k % HALF) * UNIT
                    for j, (start, part) in enumerate(passes):
                        for n in range(2):
                            last = pe.matmul(ps[i % 4][:, n, :], x3_split(i, k, start, P),
                                             ring[:, bass.ds(off + (part * D + n * 512), 512)],
                                             start=(k == 0 and j == 0),
                                             stop=(k == KT - 1 and j == len(passes) - 1))
                    last.then_inc(s("steps"), 1)

            def slot(i, mine):
                pe.wait_ge(s("s_lo"), i + 2 if i else 1)
                if i >= 4:
                    pe.wait_ge(s("staged"), i - 3)
                for half in range(2):
                    with pe.If(mine[2] < 1):
                        products(i, mine, ((0, 0), (0, 1), (P, 0)), half)
                    with pe.If(mine[2] > 0):
                        products(i, mine, ((T, 0), (T, 1)), half)
                    if half == 0 and i + 1 < SLOTS:
                        following = slot_record(i + 1)
                return following if i + 1 < SLOTS else None

            pe.wait_ge(s("plan"), 1)
            n_slots = head(pe, N_SLOTS, SURE, SLOTS)
            mine = slot_record(0)
            for i in range(SURE):
                mine = slot(i, mine)
            with contextlib.ExitStack() as nested:
                for i in range(SURE, SLOTS):
                    nested.enter_context(pe.If(n_slots > i))
                    mine = slot(i, mine)


_OUT = (B, T, D)


def kernel(x, itok_B_0_15, itok_B_0_2, itok_B_3_7, L0_cond_weights, L1_cond_weights, L2_cond_W,
           L2_cond_lora_A, L2_cond_lora_B_w, L3_cond_weight):
    import concourse.bacc as bacc
    from concourse.bass_utils import run_bass_kernel_spmd

    lay = np.ascontiguousarray
    small, before, eye = constants()
    w0 = np.asarray(L0_cond_weights).transpose(2, 0, 1)
    w1 = np.asarray(L1_cond_weights).transpose(1, 0, 2)
    la = np.asarray(L2_cond_lora_A).reshape(NL, KT, P, R).transpose(0, 2, 1, 3)
    lb = np.asarray(L2_cond_lora_B_w).transpose(1, 0)
    arrays = {
        "x": lay(x),
        "indices": lay(np.stack([np.asarray(i) for i in (itok_B_0_15, itok_B_0_2, itok_B_3_7)]).reshape(1, 3, B)),
        "w0t": lay(np.concatenate([w0[:, :, None, :]] * 2, axis=2).reshape(T, 2, D)),
        "w1": lay(w1.reshape(T, NC_ * T)),
        "wt": lay(np.asarray(L2_cond_W).transpose(1, 0)),
        "lora_a": lay(la.reshape(NL, P, KT * R)),
        "lora_b": lay(np.concatenate([lb] * (P // R), axis=0)),
        "w3t": lay(np.asarray(L3_cond_weight).transpose(0, 2, 1)),
        "small_c": small, "before_c": before, "eye_c": eye,
    }
    nc = bacc.Bacc("TRN2", target_bir_lowering=False, num_devices=1, dynamic_dma_scratch_size=1024)
    args = {n: nc.dram_tensor(n, a.shape, mybir.dt.from_np(a.dtype), kind="ExternalInput").ap() for n, a in arrays.items()}
    args["out"] = nc.dram_tensor("out", _OUT, F32, kind="ExternalOutput").ap()
    build(nc, **args)
    return run_bass_kernel_spmd(nc, [arrays], core_ids=[0]).results[0]["out"]
```
